# Optimizing a Trainium2 kernel written in Bass

```python
import numpy as np
import jax
import jax.numpy as jnp

def _softmax(x, axis=-1):
    return jax.nn.softmax(x, axis=axis)

def _gelu(x):
    return jax.nn.gelu(x, approximate=True)

def _silu(x):
    return jax.nn.silu(x)

def _sigmoid(x):
    return jax.nn.sigmoid(x)

def _layernorm(x, axis=-1, eps=1e-05):
    m = jnp.mean(x, axis=axis, keepdims=True)
    v = jnp.var(x, axis=axis, keepdims=True)
    return (x - m) / jnp.sqrt(v + eps)

def _scatter_add(tgt, idx, src, axis=0):
    return tgt.at[idx].add(src)

def _segment_sum(src, seg, n):
    return jax.ops.segment_sum(src, seg, n)
kernel_name = 'mk_decoder_postln_d1_seqx_r8_3276b5'

def setup_inputs(seed: int=0):
    np.random.seed(seed)
    _w = jnp.asarray

    def _rec_inputs():
        import jax
        import jax.numpy as jnp
        _rk = jax.random.key(seed)
        x = -0.0002928 + 1 * jax.random.normal(jax.random.fold_in(_rk, 1), (8, 128, 128), jnp.float32)
        _lenS = 128 - jax.random.randint(jax.random.fold_in(_rk, 7), (8,), 0, max(1, 128 // 4) + 1, jnp.int32)
        _lenS2 = 77 - jax.random.randint(jax.random.fold_in(_rk, 8), (8,), 0, max(1, 77 // 4) + 1, jnp.int32)
        _ctx_1024P = jax.random.normal(jax.random.fold_in(_rk, 11), (8, 16, 128), jnp.float32)
        _ctx_1024c = jax.random.dirichlet(jax.random.fold_in(_rk, 511), 0.3 * jnp.ones((16,), jnp.float32), (8, 77))
        _ctx_1024t = jnp.einsum('bsk,bkd->bsd', _ctx_1024c, _ctx_1024P)
        _ctx_1024t = _ctx_1024t * jax.lax.rsqrt(jnp.mean(jnp.square(_ctx_1024t)) + 1e-12) * 0.953939
        ctx_1024 = -1.39393e-06 + 0.999914 * (_ctx_1024t + 0.3 * jax.random.normal(jax.random.fold_in(_rk, 611), (8, 77, 128), jnp.float32))
        return (x, ctx_1024)
    x, ctx_1024 = _rec_inputs()

    def _L0_attn_setup():
        import jax, jax.numpy as jnp
        import numpy as np
        B, S, D, H, W = (2, 256, 128, 16, 32)
        HD = D // H
        key = jax.random.key(seed)
        k1, k2, k3 = jax.random.split(key, 3)
        x = jax.random.normal(k1, (B, S, D), dtype=jnp.float32)
        w_qkv = jax.random.normal(k2, (D, 3 * D), dtype=jnp.float32) * D ** (-0.5)
        b_qkv = jnp.zeros((3 * D,), dtype=jnp.float32)
        w_out = jax.random.normal(k3, (D, D), dtype=jnp.float32) * D ** (-0.5)
        b_out = jnp.zeros((D,), dtype=jnp.float32)
        return {'x': x, 'w_qkv': w_qkv, 'b_qkv': b_qkv, 'w_out': w_out, 'b_out': b_out}
    _L0_attn_all = _L0_attn_setup()
    _L0_attn_in = {k: v for k, v in _L0_attn_all.items() if k in ('w_qkv', 'b_qkv', 'w_out', 'b_out')}
    del _L0_attn_all

    def _L0_xattn_setup():
        import jax, jax.numpy as jnp
        import numpy as np
        D_MODEL = 128
        NUM_HEADS = 16
        HEAD_DIM = D_MODEL // NUM_HEADS

        def _split_heads(x):
            B, S, _ = x.shape
            return x.reshape(B, S, NUM_HEADS, HEAD_DIM).transpose(0, 2, 1, 3)
        key = jax.random.key(seed)
        ks = jax.random.split(key, 11)
        B, S = (2, 256)
        s = 1.0 / np.sqrt(D_MODEL)
        inp = {'query': jax.random.normal(ks[0], (B, S, D_MODEL), jnp.float32), 'key': jax.random.normal(ks[1], (B, S, D_MODEL), jnp.float32), 'value': jax.random.normal(ks[2], (B, S, D_MODEL), jnp.float32), 'Wq': jax.random.normal(ks[3], (D_MODEL, D_MODEL), jnp.float32) * s, 'bq': jnp.zeros((D_MODEL,), jnp.float32), 'Wk': jax.random.normal(ks[4], (D_MODEL, D_MODEL), jnp.float32) * s, 'bk': jnp.zeros((D_MODEL,), jnp.float32), 'Wv': jax.random.normal(ks[5], (D_MODEL, D_MODEL), jnp.float32) * s, 'bv': jnp.zeros((D_MODEL,), jnp.float32), 'Wo': jax.random.normal(ks[6], (D_MODEL, D_MODEL), jnp.float32) * s, 'bo': jnp.zeros((D_MODEL,), jnp.float32)}
        return inp
    _L0_xattn_all = _L0_xattn_setup()
    _L0_xattn_in = {k: v for k, v in _L0_xattn_all.items() if k in ('Wq', 'bq', 'Wk', 'bk', 'Wv', 'bv', 'Wo', 'bo')}
    del _L0_xattn_all

    def _L0_ffn_setup():
        import jax, jax.numpy as jnp
        import numpy as np
        NUM_EXPERTS = 8
        N_EMBD = 128
        D_FF = 4 * N_EMBD
        B, S = (4, 256)
        key = jax.random.key(seed)
        ks = jax.random.split(key, 6)
        x = jax.random.normal(ks[0], (B, S, N_EMBD), dtype=jnp.float32)
        gate_w = jax.random.normal(ks[1], (N_EMBD, NUM_EXPERTS), dtype=jnp.float32) * 0.02
        w1 = jax.random.normal(ks[2], (NUM_EXPERTS, N_EMBD, D_FF), dtype=jnp.float32) * 0.02
        b1 = jnp.zeros((NUM_EXPERTS, D_FF), dtype=jnp.float32)
        w2 = jax.random.normal(ks[3], (NUM_EXPERTS, D_FF, N_EMBD), dtype=jnp.float32) * 0.02
        b2 = jnp.zeros((NUM_EXPERTS, N_EMBD), dtype=jnp.float32)
        return {'x': x, 'gate_w': gate_w, 'w1': w1, 'b1': b1, 'w2': w2, 'b2': b2}
    _L0_ffn_all = _L0_ffn_setup()
    _L0_ffn_in = {k: v for k, v in _L0_ffn_all.items() if k in ('gate_w', 'w1', 'b1', 'w2', 'b2')}
    del _L0_ffn_all
    return {'x': x, 'ctx_1024': ctx_1024, 'L0_attn_w_qkv': _L0_attn_in['w_qkv'], 'L0_attn_b_qkv': _L0_attn_in['b_qkv'], 'L0_attn_w_out': _L0_attn_in['w_out'], 'L0_attn_b_out': _L0_attn_in['b_out'], 'L0_xattn_Wq': _L0_xattn_in['Wq'], 'L0_xattn_bq': _L0_xattn_in['bq'], 'L0_xattn_Wk': _L0_xattn_in['Wk'], 'L0_xattn_bk': _L0_xattn_in['bk'], 'L0_xattn_Wv': _L0_xattn_in['Wv'], 'L0_xattn_bv': _L0_xattn_in['bv'], 'L0_xattn_Wo': _L0_xattn_in['Wo'], 'L0_xattn_bo': _L0_xattn_in['bo'], 'L0_ffn_gate_w': _L0_ffn_in['gate_w'], 'L0_ffn_w1': _L0_ffn_in['w1'], 'L0_ffn_b1': _L0_ffn_in['b1'], 'L0_ffn_w2': _L0_ffn_in['w2'], 'L0_ffn_b2': _L0_ffn_in['b2']}

def reference(x, ctx_1024, L0_attn_w_qkv, L0_attn_b_qkv, L0_attn_w_out, L0_attn_b_out, L0_xattn_Wq, L0_xattn_bq, L0_xattn_Wk, L0_xattn_bk, L0_xattn_Wv, L0_xattn_bv, L0_xattn_Wo, L0_xattn_bo, L0_ffn_gate_w, L0_ffn_w1, L0_ffn_b1, L0_ffn_w2, L0_ffn_b2):
    import jax
    import jax.numpy as jnp

    def _L0_attn_ref(x, w_qkv, b_qkv, w_out, b_out):
        import jax, jax.numpy as jnp
        import numpy as np
        B, S, D, H, W = (2, 256, 128, 16, 32)
        HD = D // H
        b, s, d = x.shape
        qkv = x @ w_qkv + b_qkv
        qkv = qkv.reshape(b, s, 3, H, HD)
        q = jnp.transpose(qkv[:, :, 0], (0, 2, 1, 3))
        k = jnp.transpose(qkv[:, :, 1], (0, 2, 1, 3))
        v = jnp.transpose(qkv[:, :, 2], (0, 2, 1, 3))
        scores = jnp.einsum('bhqd,bhkd->bhqk', q, k) / d ** 0.5
        idx = jnp.arange(s)
        band = jnp.abs(idx[:, None] - idx[None, :]) <= W
        scores = jnp.where(band[None, None], scores, -jnp.inf)
        attn = jax.nn.softmax(scores, axis=-1)
        out = jnp.einsum('bhqk,bhkd->bhqd', attn, v)
        out = jnp.transpose(out, (0, 2, 1, 3)).reshape(b, s, d)
        return out @ w_out + b_out

    def _L0_xattn_ref(query, key, value, Wq, bq, Wk, bk, Wv, bv, Wo, bo):
        import jax, jax.numpy as jnp
        import numpy as np
        D_MODEL = 128
        NUM_HEADS = 16
        HEAD_DIM = D_MODEL // NUM_HEADS

        def _split_heads(x):
            B, S, _ = x.shape
            return x.reshape(B, S, NUM_HEADS, HEAD_DIM).transpose(0, 2, 1, 3)
        Q = _split_heads(query @ Wq.T + bq)
        K = _split_heads(key @ Wk.T + bk)
        V = _split_heads(value @ Wv.T + bv)
        scale = 1.0 / jnp.sqrt(jnp.asarray(HEAD_DIM, jnp.float32))
        scores = jnp.einsum('bhqd,bhkd->bhqk', Q, K) * scale
        weights = jax.nn.softmax(scores, axis=-1)
        attn = jnp.einsum('bhqk,bhkd->bhqd', weights, V)
        B, H, S, d = attn.shape
        attn = attn.transpose(0, 2, 1, 3).reshape(B, S, H * d)
        return attn @ Wo.T + bo

    def _L0_ffn_ref(x, gate_w, w1, b1, w2, b2):
        import jax, jax.numpy as jnp
        import numpy as np
        NUM_EXPERTS = 8
        N_EMBD = 128
        D_FF = 4 * N_EMBD
        B, S = (4, 256)
        Bb, Ss, D = x.shape
        x_flat = x.reshape(-1, D)
        router_logits = x_flat @ gate_w
        router_probs = jax.nn.softmax(router_logits, axis=-1)
        expert_idx = jnp.argmax(router_probs, axis=-1)
        expert_w = jnp.take_along_axis(router_probs, expert_idx[:, None], axis=1)[:, 0]
        out = jnp.zeros_like(x_flat)
        for e in range(NUM_EXPERTS):
            h = jax.nn.gelu(x_flat @ w1[e] + b1[e], approximate=False)
            y = h @ w2[e] + b2[e]
            sel = expert_idx == e
            out = out + jnp.where(sel, expert_w, 0.0)[:, None] * y
        return out.reshape(Bb, Ss, D)
    x = _layernorm(x + _L0_attn_ref(x, L0_attn_w_qkv, L0_attn_b_qkv, L0_attn_w_out, L0_attn_b_out), axis=-1)
    x = _layernorm(x + _L0_xattn_ref(x, ctx_1024, ctx_1024, L0_xattn_Wq, L0_xattn_bq, L0_xattn_Wk, L0_xattn_bk, L0_xattn_Wv, L0_xattn_bv, L0_xattn_Wo, L0_xattn_bo), axis=-1)
    x = _layernorm(x + _L0_ffn_ref(x, L0_ffn_gate_w, L0_ffn_w1, L0_ffn_b1, L0_ffn_w2, L0_ffn_b2), axis=-1)
    return x

_drawn_inputs = setup_inputs


def setup_inputs(seed=0):
    import zlib

    import numpy as np

    out = dict(_drawn_inputs(seed))
    spreads = {'L0_attn_b_qkv': (0.0, 0.1),
     'L0_attn_b_out': (0.0, 0.1),
     'L0_xattn_bq': (0.0, 0.373),
     'L0_xattn_bk': (0.0, 0.8),
     'L0_xattn_bv': (0.0, 0.1),
     'L0_xattn_bo': (0.0, 0.1),
     'L0_ffn_b1': (0.0, 0.8),
     'L0_ffn_b2': (0.0, 0.482)}
    factors = {'L0_ffn_gate_w': 3.093, 'L0_ffn_w1': 6.201, 'L0_ffn_w2': 5.626}
    for name, (base, spread) in spreads.items():
        noise = np.random.default_rng([zlib.crc32(name.encode()), seed]).standard_normal(out[name].shape)
        drawn = base * np.exp(spread * noise) if base else spread * noise
        out[name] = jnp.asarray(drawn.astype(out[name].dtype))
    for name, factor in factors.items():
        out[name] = (out[name] * factor).astype(out[name].dtype)
    return out
```

```python
from contextlib import ExitStack

import concourse.bass as bass
from concourse import mybir

F32 = mybir.dt.float32
F32R = mybir.dt.float32r
BF16 = mybir.dt.bfloat16
ACT = mybir.ActivationFunctionType
ALU = mybir.AluOpType
AX = mybir.AxisListType

P = 128
B, S, D = 8, 128, 128
H, HD = 16, 8
G, J = 4, 4
R = J * HD
SK = 77
SKP = 80
BAND = 32
E, FF = 8, 512
FC = FF // P
EPS = 1e-5
MASKED = -1e30


class Chain:
    pass


def build(nc, t, out):
    with ExitStack() as ctx:
        def sb(name, shape, dt=F32):
            return ctx.enter_context(nc.sbuf_tensor(name, shape, dt))

        def sem(name):
            return ctx.enter_context(nc.semaphore(name))

        ps = {n: ctx.enter_context(nc.psum_tensor(n, [P, k, 512], F32))
              for n, k in (("ps_scores_s", 2), ("ps_scores_c", 2), ("ps_prob_t", 2), ("ps_misc_s", 1), ("ps_misc_c", 1))}
        prob_t_ps = ps["ps_prob_t"]

        ident = sb("ident", [P, P])
        ident_bf = sb("ident_bf", [P, P], BF16)
        ones = sb("ones", [P, P])
        band4 = sb("band4", [P, J, S], BF16)
        sel = {n: sb("sel_" + n, [P, G, 4, R], F32R) for n in ("q1", "q2", "k1", "k2")}
        head_mask = sb("head_mask", [P, J])
        neg_half = sb("neg_half", [P, 1])

        w_qkv = sb("w_qkv", [D, 3 * D])
        w_out = sb("w_out", [D, D])
        w_cross = sb("w_cross", [D, 4, D])
        w_cross_t = sb("w_cross_t", [D, 4, D])
        bias_cols = sb("bias_cols", [P, 4])
        bias_rows = sb("bias_rows", [P, 4, D])
        b1_rows = sb("b1_rows", [E * FC, P])
        b1_t = sb("b1_t", [P, E * FC])
        b1_cur = sb("b1_cur", [P, FC])
        b2_rows = sb("b2_rows", [E, D])
        gate_w = sb("gate_w", [D, E])
        w1 = sb("w1", [D, 2, FF])
        w2 = sb("w2", [P, 2, FC, D])

        s_consts_pool = sem("s_consts_pool")
        s_consts_dve = sem("s_consts_dve")
        s_weights = sem("s_weights")
        s_wt_ps = sem("s_wt_ps")
        s_wt_sb = sem("s_wt_sb")

        def chain(name, n_keys, scale, masked, bias_at):
            c = Chain()
            c.n_keys, c.kp, c.scale, c.masked, c.bias_at = n_keys, n_keys + (-n_keys) % 16, scale, masked, bias_at
            c.scores = ps["ps_scores_" + name]
            c.misc = ps["ps_misc_" + name][:, 0, :]
            c.x = sb("x_" + name, [S, D])
            c.x_bo = sb("x_bo_" + name, [S, D])
            c.xt = sb("xt_" + name, [D, S])
            c.q = [sb(f"q{i}_{name}", [P, S], F32R) for i in (1, 2)]
            c.k = [sb(f"k{i}_{name}", [P, c.kp], F32R) for i in (1, 2)]
            c.v = sb("v_" + name, [n_keys, H, 32])
            c.qs = sb("qs_" + name, [P, G, S], F32R)
            c.ks = sb("ks_" + name, [P, G, c.kp])
            c.kx = sb("kx_" + name, [P, G, J, n_keys], F32R)
            c.mx = sb("mx_" + name, [S, H])
            c.prob = sb("prob_" + name, [S, H, n_keys])
            c.prob_t = sb("prob_t_" + name, [n_keys, G, J, S])
            c.av = sb("av_" + name, [P, G, S])
            c.rden = sb("rden_" + name, [S, H])
            c.att = sb("att_" + name, [S, D])
            c.att_t = sb("att_t_" + name, [D, S])
            c.res = sb("res_" + name, [S, D])
            c.stats = sb("stats_" + name, [S, 6])
            c.mv = sb("mv_" + name, [S, 2])
            c.var_eps = sb("var_eps_" + name, [S, 1])
            c.rstd = sb("rstd_" + name, [S, 1])
            c.s_loaded = sem(name + "_loaded")
            c.s_in_t_ps = sem(name + "_in_t_ps")
            c.s_in_t_sb = sem(name + "_in_t_sb")
            c.s_proj_ps = sem(name + "_proj_ps")
            c.s_part1 = sem(name + "_part1")
            c.s_parts = sem(name + "_parts")
            c.s_rep_ps = sem(name + "_rep_ps")
            c.s_qs = sem(name + "_qs")
            c.s_ks = sem(name + "_ks")
            c.s_kx = sem(name + "_kx")
            c.s_scores = sem(name + "_scores")
            c.s_mx = sem(name + "_mx")
            c.s_shifted = sem(name + "_shifted")
            c.s_prob = sem(name + "_prob")
            c.s_prob_t_ps = sem(name + "_prob_t_ps")
            c.s_prob_t_sb = sem(name + "_prob_t_sb")
            c.s_av_ps = sem(name + "_av_ps")
            c.s_av_sb = sem(name + "_av_sb")
            c.s_av_back = sem(name + "_av_back")
            c.s_rden = sem(name + "_rden")
            c.s_att = sem(name + "_att")
            c.s_att_t_ps = sem(name + "_att_t_ps")
            c.s_att_t_sb = sem(name + "_att_t_sb")
            c.s_out_ps = sem(name + "_out_ps")
            c.s_x_bo = sem(name + "_x_bo")
            c.s_res = sem(name + "_res")
            c.s_stats = sem(name + "_stats")
            c.s_mv = sem(name + "_mv")
            c.s_var_eps = sem(name + "_var_eps")
            c.s_rstd = sem(name + "_rstd")
            c.s_normed = sem(name + "_normed")
            return c

        self_ = chain("s", S, D ** -0.5, True, 0)
        cross = chain("c", SK, HD ** -0.5, False, 2)
        self_.kv_t = self_.xt
        cross.ctx = sb("ctx_cur", [SK, D])
        cross.kv_t = sb("ctx_t", [D, cross.kp])
        self_.w = (w_qkv[:, 0:D], w_qkv[:, D:2 * D], w_qkv[:, 2 * D:], w_out[:])
        cross.w = tuple(w_cross_t[:, i, :] for i in range(4))
        x2 = sb("x2", [S, D])
        x2_all = sb("x2_all", [S, B, D])
        x2_t = sb("x2_t", [D, B, S])
        s_ctx_loaded = sem("s_ctx_loaded")
        s_x2_t_ps = sem("s_x2_t_ps")
        s_x2_t_sb = sem("s_x2_t_sb")
        s_x2_kept = sem("s_x2_kept")

        logits = sb("logits", [P, B, E])
        gates = sb("gates", [P, B, E])
        rt = [sb(f"route{i}", [P, B, E]) for i in range(3)]
        rs = [sb(f"route_s{i}", [P, B]) for i in range(4)]
        rank = sb("rank", [P, E])
        rank_i = sb("rank_i", [P, E], mybir.dt.int32)
        gates_t = sb("gates_t", [E, B, P])
        hid = sb("hid", [P, 2, FC, 512])
        acc = sb("acc", [P, B, D])
        fin = sb("fin", [P, B, D])
        fstats = sb("fstats", [P, B, 6])
        fmv = sb("fmv", [P, B, 2])
        fve = sb("fve", [P, B])
        frstd = sb("frstd", [P, B])
        s_logits_ps = sem("s_logits_ps")
        s_route = sem("s_route")
        s_route_e = sem("s_route_e")
        s_gates = sem("s_gates")
        s_gates_t_ps = sem("s_gates_t_ps")
        s_gates_t_sb = sem("s_gates_t_sb")
        s_b2_ps = sem("s_b2_ps")
        s_acc = sem("s_acc")
        s_w_loaded = [sem(f"s_w_loaded{i}") for i in range(2)]
        s_up_ps = sem("s_up_ps")
        s_b1_cur = sem("s_b1_cur")
        s_hid = sem("s_hid")
        s_down_ps = sem("s_down_ps")
        s_fin = sem("s_fin")
        s_fpow = sem("s_fpow")
        s_out = sem("s_out")
        up_ps = [ps["ps_scores_s"][:, 0, :], ps["ps_scores_s"][:, 1, :], ps["ps_scores_c"][:, 0, :], ps["ps_scores_c"][:, 1, :]]
        down_ps = [ps["ps_prob_t"][:, i, :].rearrange("p (t d) -> p t d", t=4) for i in range(2)]

        block = ctx.enter_context(nc.Block())
        N_WEIGHTS = 16 * 17

        @block.sync
        def _(sp):
            sp.dma_start(self_.x[:], t["x"][0]).then_inc(self_.s_loaded, 16)
            sp.dma_start(w_qkv[:], t["L0_attn_w_qkv"]).then_inc(s_weights, 16)
            sp.dma_start(w_out[:], t["L0_attn_w_out"]).then_inc(s_weights, 16)
            for i, n in enumerate(("Wq", "Wk", "Wv", "Wo")):
                sp.dma_start(w_cross[:, i, :], t["L0_xattn_" + n]).then_inc(s_weights, 16)
            b_qkv = t["L0_attn_b_qkv"]
            col = lambda v: v.rearrange("(p a) -> p a", a=1)
            row = lambda v: v.rearrange("(a d) -> a d", a=1).broadcast_to([P, D])
            for i, v in enumerate((b_qkv[0:D], b_qkv[D:2 * D], t["L0_xattn_bq"], t["L0_xattn_bk"])):
                sp.dma_start(bias_cols[:, i:i + 1], col(v)).then_inc(s_weights, 16)
            for i, v in enumerate((b_qkv[2 * D:], t["L0_attn_b_out"], t["L0_xattn_bv"], t["L0_xattn_bo"])):
                sp.dma_start(bias_rows[:, i, :], row(v)).then_inc(s_weights, 16)
            sp.dma_start(b1_rows[:], t["L0_ffn_b1"].rearrange("e (c p) -> (e c) p", p=P)).then_inc(s_weights, 16)
            sp.dma_start(b2_rows[:], t["L0_ffn_b2"]).then_inc(s_weights, 16)
            sp.dma_start(gate_w[:], t["L0_ffn_gate_w"]).then_inc(s_weights, 16)
            sp.dma_start(cross.ctx[:], t["ctx_1024"][0]).then_inc(s_ctx_loaded, 16)

            def load_expert(e, slot):
                sp.dma_start(w1[:, slot, :], t["L0_ffn_w1"][bass.ds(e, 1)].rearrange("e d f -> d (e f)")).then_inc(s_w_loaded[slot], 16)
                sp.dma_start(w2[:, slot, :, :], t["L0_ffn_w2"][bass.ds(e, 1)].rearrange("e (c p) d -> p (e c) d", p=P)).then_inc(s_w_loaded[slot], 16)

            load_expert(0, 0)
            load_expert(1, 1)
            with sp.Fori(1, B) as b:
                sp.wait_ge(self_.s_in_t_ps, b)
                sp.wait_ge(self_.s_x_bo, b)
                sp.dma_start(self_.x[:], t["x"][bass.ds(b, 1)].rearrange("b s d -> (b s) d")).then_inc(self_.s_loaded, 16)
                sp.wait_ge(cross.s_in_t_ps, b)
                sp.dma_start(cross.ctx[:], t["ctx_1024"][bass.ds(b, 1)].rearrange("b s d -> (b s) d")).then_inc(s_ctx_loaded, 16)
            with sp.Fori(1, E // 2) as p:
                for slot in range(2):
                    sp.wait_ge(s_down_ps, 4 * p + 2 * slot - 2)
                    load_expert(2 * p + slot, slot)
            sp.wait_ge(s_fin, 1 + 1)
            sp.dma_start(out.rearrange("b s d -> s b d"), fin[:]).then_inc(s_out, 16)
            sp.wait_ge(s_out, 16)

        @block.gpsimd
        def _(pool):
            g = nc.gpsimd
            g.memset(ones[:], 1.0).then_inc(s_consts_pool, 1)
            g.memset(band4[:], 0.0).then_inc(s_consts_pool, 1)
            g.memset(neg_half[:], -0.5).then_inc(s_consts_pool, 1)
            g.iota(rank_i[:], pattern=[[-1, E]], base=E, channel_multiplier=0).then_inc(s_consts_pool, 1)
            pool.wait_ge(s_consts_pool, 2)
            g.affine_select(out=ident[:], in_=ones[:], compare_op=ALU.is_equal, fill=0.0, base=0,
                            pattern=[[-1, P]], channel_multiplier=1).then_inc(s_consts_pool, 1)
            g.affine_select(out=band4[:], in_=band4[:], compare_op=ALU.is_ge, fill=MASKED, base=BAND,
                            pattern=[[0, J], [1, S]], channel_multiplier=-1).then_inc(s_consts_pool, 1)
            pool.wait_ge(s_consts_pool, 6)
            g.affine_select(out=band4[:], in_=band4[:], compare_op=ALU.is_ge, fill=MASKED, base=BAND,
                            pattern=[[0, J], [-1, S]], channel_multiplier=1).then_inc(s_consts_pool, 1)
            g.tensor_copy(rank[:], rank_i[:]).then_inc(s_consts_pool, 1)

            def residual(c, b):
                pool.wait_ge(c.s_loaded if c is self_ else self_.s_normed, (b + 1) * (16 if c is self_ else 1))
                if not isinstance(b, int) or b:
                    pool.wait_ge(c.s_res, b)
                g.tensor_tensor(c.x_bo[:], c.x[:], bias_rows[:, c.bias_at + 1, :], ALU.add).then_inc(c.s_x_bo, 1)

            def power(c, b):
                pool.wait_ge(c.s_var_eps, b + 1)
                g.tensor_tensor(c.rstd[:], c.var_eps[:], neg_half[:], ALU.pow).then_inc(c.s_rstd, 1)

            def keep(b):
                pool.wait_ge(cross.s_normed, b + 1)
                g.tensor_copy(x2_all[:, bass.ds(b, 1), :], x2[:].rearrange("p (a d) -> p a d", a=1)).then_inc(s_x2_kept, 1)

            pool.wait_ge(s_weights, N_WEIGHTS)
            residual(self_, 0)
            power(self_, 0)
            residual(self_, 1)
            residual(cross, 0)
            power(self_, 1)
            power(cross, 0)
            keep(0)
            with pool.Fori(2, B) as i:
                residual(self_, i)
                residual(cross, i - 1)
                power(self_, i)
                power(cross, i - 1)
                keep(i - 1)
            residual(cross, B - 1)
            power(cross, B - 1)
            keep(B - 1)
            pool.wait_ge(s_fpow, 1)
            g.tensor_tensor(frstd[:], fve[:], neg_half[:].broadcast_to([P, B]), ALU.pow).then_inc(s_fpow, 1)

        @block.tensor
        def _(pe):
            mm, tr = nc.tensor.matmul, nc.tensor.transpose

            def inputs(c, b):
                m = c.misc
                if c is self_:
                    pe.wait_ge(c.s_loaded, 16 * b + 16)
                    if not isinstance(b, int) or b:
                        pe.wait_ge(c.s_res, b)
                    tr(m[:, 0:S], c.x[:], ident[:]).then_inc(c.s_in_t_ps, 1)
                else:
                    pe.wait_ge(self_.s_normed, b + 1)
                    pe.wait_ge(s_ctx_loaded, 16 * b + 16)
                    pe.wait_ge(s_x2_t_sb, b + 1)
                    tr(m[:, 0:S], c.x[:], ident[:])
                    tr(m[:, S:S + SK], c.ctx[:], ident[0:SK, 0:SK]).then_inc(c.s_in_t_ps, 1)
                pe.wait_ge(c.s_in_t_sb, b + 1)
                wq, wk, wv, _ = c.w
                mm(m[:, 0:S], wq, c.xt[:], start=True, stop=True)
                mm(m[:, S:S + c.kp], wk, c.kv_t[:], start=True, stop=True)
                mm(m[0:c.n_keys, 2 * S:3 * S], c.kv_t[:, 0:c.n_keys], wv, start=True, stop=True).then_inc(c.s_proj_ps, 1)

            def operands(c, b):
                pe.wait_ge(c.s_parts, 2 * b + 2)
                for parts, sels, bank, w in ((c.q, ("q1", "q2"), 0, S), (c.k, ("k1", "k2"), 1, c.kp)):
                    for g in range(G):
                        o = c.scores[:, bank, g * w:(g + 1) * w]
                        for i in range(2):
                            last = mm(o, sel[sels[i]][:, g, :, :].rearrange("p t r -> p (t r)"), parts[i][:],
                                      start=i == 0, stop=i == 1)
                    last.then_inc(c.s_rep_ps, 1)

            def scores(c, b, half):
                if half == 0:
                    pe.wait_ge(c.s_qs, b + 1)
                    pe.wait_ge(c.s_kx, b + 1)
                else:
                    pe.wait_ge(c.s_shifted, 2 * b + 1)
                for n in range(2):
                    g = 2 * half + n
                    o = c.scores[:, n, 0:J * c.n_keys]
                    last = mm(o, c.qs[:, g, :], c.kx[:, g, :, :].rearrange("p j k -> p (j k)"), start=True, stop=not c.masked)
                    if c.masked:
                        last = mm(o, ident_bf[:], band4[:].rearrange("p j k -> p (j k)"), start=False, stop=True)
                last.then_inc(c.s_scores, 1)

            def values(c, b, half):
                pe.wait_ge(c.s_prob, 2 * b + half + 1)
                for n in range(2):
                    for j in range(J):
                        h = (2 * half + n) * J + j
                        last = tr(prob_t_ps[0:c.n_keys, n, j * S:(j + 1) * S], c.prob[:, h, :], ident[:])
                    last.then_inc(c.s_prob_t_ps, 1)
                for n in range(2):
                    g = 2 * half + n
                    pe.wait_ge(c.s_prob_t_sb, 4 * b + g + 1)
                    for j in range(J):
                        last = mm(c.misc[32 * j:32 * j + 32, g * S:(g + 1) * S], c.v[:, g * J + j, :], c.prob_t[:, g, j, :],
                                  start=True, stop=True, tile_position=(0, 32 * j))
                    last.then_inc(c.s_av_ps, 1)

            def output(c, b):
                pe.wait_ge(c.s_av_sb, b + 1)
                for g in range(G):
                    last = tr(c.scores[:, 0, g * S:(g + 1) * S], c.av[:, g, :], ident[:])
                last.then_inc(c.s_av_back, 1)
                pe.wait_ge(c.s_att, b + 1)
                tr(c.misc[:, 0:S], c.att[:], ident[:]).then_inc(c.s_att_t_ps, 1)
                pe.wait_ge(c.s_att_t_sb, b + 1)
                mm(c.misc[:, S:S + D], c.att_t[:], c.w[3], start=True, stop=True).then_inc(c.s_out_ps, 1)

            def keep_transposed(b):
                pe.wait_ge(cross.s_normed, b + 1)
                tr(cross.misc[:, 0:S], x2[:], ident[:]).then_inc(s_x2_t_ps, 1)

            def both(i, with_self=True, with_cross=True, with_next=True):
                if with_self:
                    scores(self_, i, 0)
                if with_cross:
                    inputs(cross, i - 1)
                    operands(cross, i - 1)
                if with_self:
                    scores(self_, i, 1)
                if with_cross:
                    scores(cross, i - 1, 0)
                if with_self:
                    values(self_, i, 0)
                if with_cross:
                    scores(cross, i - 1, 1)
                if with_self:
                    values(self_, i, 1)
                if with_cross:
                    values(cross, i - 1, 0)
                if with_self:
                    output(self_, i)
                if with_next:
                    inputs(self_, i + 1)
                    operands(self_, i + 1)
                if with_cross:
                    values(cross, i - 1, 1)
                    output(cross, i - 1)
                    keep_transposed(i - 1)

            pe.wait_ge(s_consts_pool, 8)
            pe.wait_ge(s_consts_dve, 13)
            pe.wait_ge(s_weights, N_WEIGHTS)
            for i in range(4):
                tr(cross.misc[:, i * D:(i + 1) * D], w_cross[:, i, :], ident[:])
            tr(cross.scores[:, 0, 0:E * FC], b1_rows[:], ident[0:E * FC, 0:E * FC]).then_inc(s_wt_ps, 1)
            pe.wait_ge(s_wt_sb, 2)
            inputs(self_, 0)
            operands(self_, 0)
            both(0, with_cross=False)
            with pe.Fori(1, B - 1) as i:
                both(i)
            both(B - 1, with_next=False)
            both(B, with_self=False, with_next=False)

            pe.wait_ge(s_x2_t_sb, B + 1)
            for b in range(B):
                last = mm(self_.misc[:, b * E:(b + 1) * E], x2_t[:, b, :], gate_w[:], start=True, stop=True)
            last.then_inc(s_logits_ps, 1)
            pe.wait_ge(s_gates, 1)
            for b in range(B):
                last = tr(cross.scores[0:E, b // 4, (b % 4) * P:(b % 4 + 1) * P], gates[:, b, :], ident[:])
            last.then_inc(s_gates_t_ps, 1)
            pe.wait_ge(s_gates_t_sb, 1)
            for b in range(B):
                last = mm(down_ps[b // 4][:, b % 4, :], gates_t[:, b, :], b2_rows[:], start=True, stop=True)
            last.then_inc(s_b2_ps, 1)
            pe.wait_ge(s_acc, 1)
            with pe.Fori(0, E // 2) as p:
                for slot in range(2):
                    e = 2 * p + slot
                    pe.wait_ge(s_w_loaded[slot], 32 * p + 32)
                    for half in range(2):
                        for c in range(FC):
                            n = half * FC + c
                            pe.wait_ge(s_hid, 8 * e + n + 1)
                            mm(up_ps[c], w1[:, slot, c * P:(c + 1) * P],
                               x2_t[:, 4 * half:4 * half + 4, :].rearrange("p b s -> p (b s)"), start=True, stop=True).then_inc(s_up_ps, 1)
                    for half in range(2):
                        pe.wait_ge(s_hid, 8 * e + 4 * half + 4 + 4)
                        pe.wait_ge(s_acc, 2 * e + half + 1)
                        for tt in range(4):
                            for c in range(FC):
                                last = mm(down_ps[half][:, tt, :], hid[:, half, c, tt * P:(tt + 1) * P], w2[:, slot, c, :],
                                          start=c == 0, stop=c == FC - 1)
                        last.then_inc(s_down_ps, 1)

        @block.scalar
        def _(act):
            copy = lambda o, i: nc.scalar.activation(o, i, ACT.Copy)

            def inputs(c, b):
                act.wait_ge(c.s_in_t_ps, b + 1)
                last = copy(c.xt[:], c.misc[:, 0:S])
                if c is cross:
                    last = copy(c.kv_t[:, 0:SK], c.misc[:, S:S + SK])
                last.then_inc(c.s_in_t_sb, 1)
                act.wait_ge(c.s_proj_ps, b + 1)
                a = c.bias_at
                nc.scalar.activation(c.q[0][:], c.misc[:, 0:S], ACT.Identity, bias=bias_cols[:, a:a + 1])
                nc.scalar.activation(c.k[0][:], c.misc[:, S:S + c.kp], ACT.Identity, bias=bias_cols[:, a + 1:a + 2]).then_inc(c.s_part1, 1)

            def operands(c, b):
                act.wait_ge(c.s_rep_ps, 2 * b + 1)
                copy(c.qs[:].rearrange("p g s -> p (g s)"), c.scores[:, 0, :]).then_inc(c.s_qs, 1)
                act.wait_ge(c.s_rep_ps, 2 * b + 2)
                copy(c.ks[:].rearrange("p g s -> p (g s)"), c.scores[:, 1, 0:G * c.kp]).then_inc(c.s_ks, 1)

            def exps(c, b, half):
                act.wait_ge(c.s_shifted, 2 * b + half + 1)
                o = c.prob[:, 8 * half:8 * half + 8, :].rearrange("p h k -> p (h k)")
                nc.scalar.activation(o, o, ACT.Exp, scale=c.scale).then_inc(c.s_prob, 1)

            def values(c, b, half):
                for n in range(2):
                    g = 2 * half + n
                    act.wait_ge(c.s_prob_t_ps, 4 * b + g + 1)
                    copy(c.prob_t[:, g, :, :].rearrange("p j s -> p (j s)"), prob_t_ps[0:c.n_keys, n, :]).then_inc(c.s_prob_t_sb, 1)

            def output(c, b):
                act.wait_ge(c.s_av_ps, 4 * b + 4)
                copy(c.av[:].rearrange("p g s -> p (g s)"), c.misc[:, :]).then_inc(c.s_av_sb, 1)
                act.wait_ge(c.s_att_t_ps, b + 1)
                copy(c.att_t[:], c.misc[:, 0:S]).then_inc(c.s_att_t_sb, 1)

            def keep_transposed(b):
                act.wait_ge(s_consts_dve, 13)
                act.wait_ge(s_x2_t_ps, b + 1)
                copy(x2_t[:, bass.ds(b, 1), :], cross.misc[:, 0:S].rearrange("p (a s) -> p a s", a=1)).then_inc(s_x2_t_sb, 1)

            def both(i, with_self=True, with_cross=True, with_next=True):
                if with_self:
                    exps(self_, i, 0)
                if with_cross:
                    inputs(cross, i - 1)
                    operands(cross, i - 1)
                if with_self:
                    exps(self_, i, 1)
                    values(self_, i, 0)
                if with_cross:
                    exps(cross, i - 1, 0)
                if with_self:
                    values(self_, i, 1)
                if with_cross:
                    exps(cross, i - 1, 1)
                    values(cross, i - 1, 0)
                if with_self:
                    output(self_, i)
                if with_next:
                    inputs(self_, i + 1)
                    operands(self_, i + 1)
                if with_cross:
                    values(cross, i - 1, 1)
                    output(cross, i - 1)
                    keep_transposed(i - 1)

            act.wait_ge(s_wt_ps, 1)
            copy(w_cross_t[:].rearrange("p a d -> p (a d)"), cross.misc[:, :]).then_inc(s_wt_sb, 1)
            copy(b1_t[:], cross.scores[:, 0, 0:E * FC]).then_inc(s_wt_sb, 1)
            act.wait_ge(s_consts_pool, 8)
            copy(ident_bf[:], ident[:]).then_inc(s_x2_t_sb, 1)
            inputs(self_, 0)
            operands(self_, 0)
            both(0, with_cross=False)
            with act.Fori(1, B - 1) as i:
                both(i)
            both(B - 1, with_next=False)
            both(B, with_self=False, with_next=False)

            act.wait_ge(s_route, 3)
            nc.scalar.activation(rt[1][:], rt[0][:], ACT.Exp).then_inc(s_route_e, 1)
            act.wait_ge(s_gates_t_ps, 1)
            copy(gates_t[:].rearrange("p b s -> p (b s)"), cross.scores[0:E, :, :].rearrange("p a s -> p (a s)")).then_inc(s_gates_t_sb, 1)
            for c in range(FC):
                copy(rs[3][0:1, 2 * c:2 * c + 1], ones[0:1, 0:1]).then_inc(s_hid, 1)
            with act.Fori(0, E) as e:
                act.wait_ge(s_hid, 8 * e + 4)
                copy(b1_cur[:], b1_t[:, bass.ds(e * FC, FC)]).then_inc(s_b1_cur, 1)
                act.wait_ge(s_b1_cur, e + 1)
                for half in range(2):
                    for c in range(FC):
                        act.wait_ge(s_up_ps, 8 * e + 4 * half + c + 1)
                        nc.scalar.activation(hid[:, half, c, :], up_ps[c], ACT.Gelu, bias=b1_cur[:, c:c + 1]).then_inc(s_hid, 1)

        @block.vector
        def _(dve):
            v = nc.vector

            def inputs(c, b):
                dve.wait_ge(c.s_part1, b + 1)
                a = c.bias_at
                v.scalar_tensor_tensor(c.q[1][:], c.misc[:, 0:S], bias_cols[:, a:a + 1], c.q[0][:].bitcast(F32), ALU.add, ALU.subtract)
                v.scalar_tensor_tensor(c.k[1][:], c.misc[:, S:S + c.kp], bias_cols[:, a + 1:a + 2], c.k[0][:].bitcast(F32),
                                       ALU.add, ALU.subtract).then_inc(c.s_parts, 1)
                n = c.n_keys
                v.tensor_tensor(c.v[:, :, 0:HD], c.misc[0:n, 2 * S:3 * S].rearrange("p (h d) -> p h d", d=HD),
                                bias_rows[0:n, a, :].rearrange("p (h d) -> p h d", d=HD), ALU.add).then_inc(c.s_parts, 1)

            def operands(c, b):
                dve.wait_ge(c.s_ks, b + 1)
                for j in range(J):
                    last = v.tensor_scalar(c.kx[:, :, j, :], c.ks[:, :, 0:c.n_keys], head_mask[:, j:j + 1], None, ALU.mult)
                last.then_inc(c.s_kx, 1)

            def softmax(c, b, half):
                dve.wait_ge(c.s_scores, 2 * b + half + 1)
                sc = c.scores[:, :, 0:J * c.n_keys].rearrange("p g (j k) -> p g j k", j=J)
                m = c.mx[:, 8 * half:8 * half + 8].rearrange("p (g j) -> p g j", j=J)
                v.tensor_reduce(m, sc, AX.X, ALU.max).then_inc(c.s_mx, 1)
                dve.wait_ge(c.s_mx, 2 * b + half + 1)
                o = c.prob[:, 8 * half:8 * half + 8, :].rearrange("p (g j) k -> p g j k", j=J)
                v.tensor_tensor(o, sc, m.unsqueeze(3).broadcast_to([S, 2, J, c.n_keys]), ALU.subtract).then_inc(c.s_shifted, 1)

            def output(c, b, to):
                dve.wait_ge(c.s_av_back, b + 1)
                back = c.scores[:, 0, :].rearrange("p (h w) -> p h w", w=32)
                v.reciprocal(c.rden[:].unsqueeze(2), back[:, :, HD:HD + 1]).then_inc(c.s_rden, 1)
                dve.wait_ge(c.s_rden, b + 1)
                v.tensor_tensor(c.att[:].rearrange("p (h d) -> p h d", d=HD), back[:, :, 0:HD],
                                c.rden[:].unsqueeze(2).broadcast_to([S, H, HD]), ALU.mult).then_inc(c.s_att, 1)
                dve.wait_ge(c.s_out_ps, b + 1)
                dve.wait_ge(c.s_x_bo, b + 1)
                v.tensor_tensor(c.res[:], c.misc[:, S:S + D], c.x_bo[:], ALU.add).then_inc(c.s_res, 1)
                dve.wait_ge(c.s_res, b + 1)
                v.bn_stats(c.stats[:], c.res[:]).then_inc(c.s_stats, 1)
                dve.wait_ge(s_route, 1)
                dve.wait_ge(c.s_stats, b + 1)
                v.bn_aggr(c.mv[:], c.stats[:]).then_inc(c.s_mv, 1)
                dve.wait_ge(c.s_mv, b + 1)
                v.tensor_scalar(c.var_eps[:], c.mv[:, 1:2], EPS, None, ALU.add).then_inc(c.s_var_eps, 1)
                dve.wait_ge(c.s_rstd, b + 1)
                if c is self_ and (not isinstance(b, int) or b):
                    dve.wait_ge(cross.s_x_bo, b)
                if c is cross and (not isinstance(b, int) or b):
                    dve.wait_ge(s_x2_kept, b)
                v.tensor_scalar(to, c.res[:], c.mv[:, 0:1], c.rstd[:, 0:1], ALU.subtract, ALU.mult).then_inc(c.s_normed, 1)

            def both(i, with_self=True, with_cross=True, with_next=True):
                if with_self:
                    softmax(self_, i, 0)
                if with_cross:
                    inputs(cross, i - 1)
                    operands(cross, i - 1)
                if with_self:
                    softmax(self_, i, 1)
                if with_cross:
                    softmax(cross, i - 1, 0)
                    softmax(cross, i - 1, 1)
                if with_self:
                    output(self_, i, cross.x[:])
                if with_next:
                    inputs(self_, i + 1)
                    operands(self_, i + 1)
                if with_cross:
                    output(cross, i - 1, x2[:])

            for c in (self_, cross):
                v.memset(c.v[:], 0.0).then_inc(s_consts_dve, 1)
            v.memset(cross.kv_t[:, SK:], 0.0).then_inc(s_consts_dve, 1)
            for n in sel:
                v.memset(sel[n][:].bitcast(F32), 0.0).then_inc(s_consts_dve, 1)
            dve.wait_ge(s_consts_dve, 7)
            dve.wait_ge(s_consts_pool, 8)
            for c in (self_, cross):
                v.memset(c.v[:, :, HD:HD + 1], 1.0).then_inc(s_consts_dve, 1)
            by_group = ident[:].rearrange("p (g r) -> p g r", r=R)
            for n, quadrants in (("q1", (0, 1)), ("q2", (2, 3)), ("k1", (0, 2)), ("k2", (1, 3))):
                for q in quadrants:
                    last = v.tensor_copy(sel[n][:, :, q, :], by_group)
                if n != "k2":
                    last.then_inc(s_consts_dve, 1)
            last.then_inc(s_consts_dve, 1)
            v.tensor_reduce(head_mask[:], ident[:].rearrange("p (q j d) -> p j q d", q=4, d=HD), AX.XY, ALU.add).then_inc(s_route, 1)
            dve.wait_ge(s_route, 1)
            inputs(self_, 0)
            operands(self_, 0)
            both(0, with_cross=False)
            with dve.Fori(1, B - 1) as i:
                both(i)
            both(B - 1, with_next=False)
            both(B, with_self=False, with_next=False)

            per_token = lambda a: a[:].unsqueeze(2).broadcast_to([P, B, E])
            dve.wait_ge(s_logits_ps, 1)
            v.tensor_copy(logits[:].rearrange("p b e -> p (b e)"), self_.misc[:, 0:B * E]).then_inc(s_route, 1)
            dve.wait_ge(s_route, 2)
            v.tensor_reduce(rs[0][:], logits[:], AX.X, ALU.max).then_inc(s_route_e, 1)
            dve.wait_ge(s_route_e, 1)
            v.tensor_tensor(rt[0][:], logits[:], per_token(rs[0]), ALU.subtract).then_inc(s_route, 1)
            dve.wait_ge(s_route, 3)
            v.tensor_scalar(rt[2][:], rt[0][:], 0.0, None, ALU.is_equal).then_inc(s_route, 1)
            dve.wait_ge(s_route_e, 2)
            v.tensor_reduce(rs[1][:], rt[1][:], AX.X, ALU.add).then_inc(s_route, 1)
            dve.wait_ge(s_route, 5)
            v.reciprocal(rs[2][:], rs[1][:]).then_inc(s_route, 1)
            v.tensor_tensor(logits[:], rt[2][:], rank[:].unsqueeze(1).broadcast_to([P, B, E]), ALU.mult).then_inc(s_route, 1)
            dve.wait_ge(s_route, 7)
            v.tensor_reduce(rs[0][:], logits[:], AX.X, ALU.max).then_inc(s_route, 1)
            dve.wait_ge(s_route, 8)
            v.tensor_tensor(rt[1][:], logits[:], per_token(rs[0]), ALU.is_equal).then_inc(s_route, 1)
            dve.wait_ge(s_route, 9)
            v.tensor_tensor(gates[:], rt[1][:], per_token(rs[2]), ALU.mult).then_inc(s_gates, 1)
            dve.wait_ge(s_b2_ps, 1)
            dve.wait_ge(s_x2_kept, B)
            for half in range(2):
                v.tensor_tensor(acc[:, 4 * half:4 * half + 4, :], down_ps[half], x2_all[:, 4 * half:4 * half + 4, :], ALU.add).then_inc(s_acc, 1)
            with dve.Fori(0, E) as e:
                for half in range(2):
                    dve.wait_ge(s_down_ps, 2 * e + half + 1)
                    dve.wait_ge(s_acc, 2 * e + half + 1)
                    for tt in range(4):
                        bt = 4 * half + tt
                        last = v.scalar_tensor_tensor(acc[:, bt, :], down_ps[half][:, tt, :], gates[:, bt, bass.ds(e, 1)], acc[:, bt, :], ALU.mult, ALU.add)
                    last.then_inc(s_acc, 1)
            dve.wait_ge(s_acc, 2 * E + 2)
            for bt in range(B):
                last = v.bn_stats(fstats[:, bt, :], acc[:, bt, :])
            last.then_inc(s_route, 1)
            dve.wait_ge(s_route, 10)
            for bt in range(B):
                last = v.bn_aggr(fmv[:, bt, :], fstats[:, bt, :])
            last.then_inc(s_route, 1)
            dve.wait_ge(s_route, 11)
            v.tensor_scalar(fve[:].unsqueeze(2), fmv[:, :, 1:2], EPS, None, ALU.add).then_inc(s_fpow, 1)
            dve.wait_ge(s_fpow, 2)
            for bt in range(B):
                last = v.tensor_scalar(fin[:, bt, :], acc[:, bt, :], fmv[:, bt, 0:1], frstd[:, bt:bt + 1], ALU.subtract, ALU.mult)
                if bt in (0, B - 1):
                    last.then_inc(s_fin, 1)


_INS = ['x', 'ctx_1024', 'L0_attn_w_qkv', 'L0_attn_b_qkv', 'L0_attn_w_out', 'L0_attn_b_out', 'L0_xattn_Wq', 'L0_xattn_bq',
        'L0_xattn_Wk', 'L0_xattn_bk', 'L0_xattn_Wv', 'L0_xattn_bv', 'L0_xattn_Wo', 'L0_xattn_bo', 'L0_ffn_gate_w',
        'L0_ffn_w1', 'L0_ffn_b1', 'L0_ffn_w2', 'L0_ffn_b2']


def kernel(**inputs):
    import numpy as _np
    import concourse.bacc as _bacc
    from concourse import mybir as _mybir
    from concourse.bass_utils import run_bass_kernel_spmd as _run

    nc = _bacc.Bacc("TRN2", target_bir_lowering=False, num_devices=1)
    arrays, aps = {}, {}
    for name in _INS:
        a = _np.ascontiguousarray(inputs[name])
        arrays[f"in_{name}"] = a
        aps[name] = nc.dram_tensor(f"in_{name}", a.shape, _mybir.dt.from_np(a.dtype), kind="ExternalInput").ap()
    out = nc.dram_tensor("out_0", (B, S, D), F32, kind="ExternalOutput").ap()
    build(nc, aps, out)
    r = _run(nc, [arrays], core_ids=[0])
    return r.results[0]["out_0"]
```

```python
from contextlib import ExitStack

import concourse.bass as bass
from concourse import mybir

F32 = mybir.dt.float32
F32R = mybir.dt.float32r
BF16 = mybir.dt.bfloat16
ACT = mybir.ActivationFunctionType
ALU = mybir.AluOpType
AX = mybir.AxisListType

P = 128
B, S, D = 8, 128, 128
H, HD = 16, 8
G, J = 4, 4
R = J * HD
SK = 77
SKP = 80
BAND = 32
E, FF = 8, 512
FC = FF // P
EPS = 1e-5
MASKED = -1e30


class Chain:
    pass


def build(nc, t, out):
    with ExitStack() as ctx:
        def sb(name, shape, dt=F32):
            return ctx.enter_context(nc.sbuf_tensor(name, shape, dt))

        def sem(name):
            return ctx.enter_context(nc.semaphore(name))

        ps = ctx.enter_context(nc.psum_tensor("ps", [P, 8, 512], F32))
        bank = lambda i: ps[:, i, :]
        PT, AV = 4, 6

        ident = sb("ident", [P, P])
        ident_bf = sb("ident_bf", [P, P], BF16)
        ones = sb("ones", [P, P])
        band4 = sb("band4", [P, J, S], BF16)
        sel_names = ("q1", "q2", "k1", "k2")
        sel = {n: sb("sel_" + n, [P, G, 4, R], F32R) for n in sel_names}
        head_mask = sb("head_mask", [P, J])
        neg_half = sb("neg_half", [P, 4])
        s_ones = sem("s_ones")
        s_ident = sem("s_ident")
        s_band_zero = sem("s_band_zero")
        s_band_half = sem("s_band_half")
        s_band = sem("s_band")
        s_neg_half = sem("s_neg_half")
        s_ident_bf = sem("s_ident_bf")
        s_zeroed = sem("s_zeroed")
        s_sel = sem("s_sel")
        s_ones_col = sem("s_ones_col")
        s_head_mask = sem("s_head_mask")

        w_qkv = sb("w_qkv", [D, 3 * D])
        w_out = sb("w_out", [D, D])
        w_cross = sb("w_cross", [D, 4, D])
        w_cross_t = sb("w_cross_t", [D, 4, D])
        bias_cols = sb("bias_cols", [P, 4])
        bias_rows = sb("bias_rows", [P, 4, D])
        b1_rows = sb("b1_rows", [E * FC, P])
        b1_t = sb("b1_t", [P, E * FC])
        b1_cur = sb("b1_cur", [P, FC])
        b2_rows = sb("b2_rows", [E, D])
        gate_w = sb("gate_w", [D, E])
        w1 = sb("w1", [D, 2, FF])
        w2 = sb("w2", [P, 2, FC, D])
        s_w_qkv = sem("s_w_qkv")
        s_small = sem("s_small")
        s_w_cross = sem("s_w_cross")
        s_w_late = sem("s_w_late")
        s_wt_ps = sem("s_wt_ps")
        s_wt_sb = sem("s_wt_sb")
        s_b1_sb = sem("s_b1_sb")

        q_parts = [sb(f"q_part{i}", [P, B * S], F32R) for i in (1, 2)]
        k_parts = [sb(f"k_part{i}", [P, B * S], F32R) for i in (1, 2)]
        qs_all = sb("qs_all", [P, G, B, S])
        ks_all = sb("ks_all", [P, G, B, S])
        av_all = sb("av_all", [P, B, G * S])
        prob = sb("prob", [S, H, S])
        prob_t = sb("prob_t", [S, G, J, S])
        qs = sb("qs", [P, 2, G, S], F32R)
        kx = sb("kx", [P, 2, G, J * S], F32R)
        v_row = sb("v_row", [P, 2, H, 32])
        mx = sb("mx", [S, H])
        rden = sb("rden", [S, B, H])
        att = sb("att", [S, B, D])
        att_t = sb("att_t", [D, B, S])
        res = sb("res", [S, B, D])
        stats = sb("stats", [S, B, 6])
        mv = sb("mv", [S, B, 2])
        var_eps = sb("var_eps", [S, B])
        rstd = sb("rstd", [S, B])

        def attention(name, n_keys, scale, masked, bias_at, x, xt, x_bo):
            c = Chain()
            c.n_keys, c.kp, c.scale, c.masked, c.bias_at = n_keys, n_keys + (-n_keys) % 16, scale, masked, bias_at
            c.x, c.xt, c.x_bo = x, xt, x_bo
            c.ks = ks_all[:, :, :, 0:c.kp]
            c.prob = prob[:].rearrange("p h k -> p (h k)")[:, 0:H * n_keys].rearrange("p (h k) -> p h k", h=H)
            c.prob_t = prob_t[0:n_keys]
            c.v_all = sb("v_all_" + name, [n_keys, B, D])
            c.qs = qs
            c.kx = kx[:].rearrange("p t g n -> p (t g n)")[:, 0:2 * H * n_keys].rearrange("p (t g j k) -> p t g j k", t=2, g=G, j=J)
            c.v = v_row[0:n_keys]
            c.s_xt_ps = sem(name + "_xt_ps")
            c.s_xt = sem(name + "_xt")
            c.s_x_bo = sem(name + "_x_bo")
            c.s_q_ps = sem(name + "_q_ps")
            c.s_q_part1 = sem(name + "_q_part1")
            c.s_q_part2 = sem(name + "_q_part2")
            c.s_k_ps = sem(name + "_k_ps")
            c.s_k_part1 = sem(name + "_k_part1")
            c.s_k_part2 = sem(name + "_k_part2")
            c.s_v_ps = sem(name + "_v_ps")
            c.s_v_all = sem(name + "_v_all")
            c.s_rep_ps = sem(name + "_rep_ps")
            c.s_rep_act = sem(name + "_rep_act")
            c.s_rep_dve = sem(name + "_rep_dve")
            c.s_qs = sem(name + "_qs")
            c.s_kx = sem(name + "_kx")
            c.s_v = sem(name + "_v")
            c.s_scores = sem(name + "_scores")
            c.s_mx = sem(name + "_mx")
            c.s_shifted = sem(name + "_shifted")
            c.s_prob = sem(name + "_prob")
            c.s_prob_t_ps = sem(name + "_prob_t_ps")
            c.s_prob_t = sem(name + "_prob_t")
            c.s_av_ps = sem(name + "_av_ps")
            c.s_av = sem(name + "_av")
            c.s_back = sem(name + "_back")
            c.s_rden = sem(name + "_rden")
            c.s_att = sem(name + "_att")
            c.s_att_t_ps = sem(name + "_att_t_ps")
            c.s_att_t = sem(name + "_att_t")
            c.s_out_ps = sem(name + "_out_ps")
            c.s_res = sem(name + "_res")
            c.s_stats = sem(name + "_stats")
            c.s_mv = sem(name + "_mv")
            c.s_var_eps = sem(name + "_var_eps")
            c.s_rstd = sem(name + "_rstd")
            c.s_normed = sem(name + "_normed")
            return c

        x0 = sb("x0", [S, B, D])
        x1 = sb("x1", [S, B, D])
        x2 = sb("x2", [S, B, D])
        xt = sb("xt", [D, B, S])
        x2_t = sb("x2_t", [D, B, S])
        x_bo = sb("x_bo", [S, B, D])
        self_ = attention("self", S, D ** -0.5, True, 0, x0, xt, x_bo)
        cross = attention("cross", SK, HD ** -0.5, False, 2, x1, xt, x_bo)
        context = sb("context", [SK, B, D])
        context_t = sb("context_t", [D, B, SKP])
        self_.kv_t, cross.kv_t = xt, context_t
        self_.w = (w_qkv[:, 0:D], w_qkv[:, D:2 * D], w_qkv[:, 2 * D:], w_out[:])
        cross.w = tuple(w_cross_t[:, i, :] for i in range(4))
        self_.to, cross.to = x1, x2
        s_x = sem("s_x")
        s_context = sem("s_context")
        s_context_t_ps = sem("s_context_t_ps")
        s_context_t = sem("s_context_t")
        s_x2_t_ps = sem("s_x2_t_ps")
        s_x2_t = sem("s_x2_t")

        logits = sb("logits", [P, B, E])
        gates = sb("gates", [P, B, E])
        rt = [sb(f"route{i}", [P, B, E]) for i in range(3)]
        rs = [sb(f"route_s{i}", [P, B]) for i in range(3)]
        rank = sb("rank", [P, E])
        rank_i = sb("rank_i", [P, E], mybir.dt.int32)
        gates_t = sb("gates_t", [E, B, P])
        hid = prob_t
        acc = x_bo
        s_rank_i = sem("s_rank_i")
        s_rank = sem("s_rank")
        s_logits_ps = sem("s_logits_ps")
        s_route = sem("s_route")
        s_route_e = sem("s_route_e")
        s_gates = sem("s_gates")
        s_gates_t_ps = sem("s_gates_t_ps")
        s_gates_t_sb = sem("s_gates_t_sb")
        s_b2_ps = sem("s_b2_ps")
        s_acc = sem("s_acc")
        s_w_loaded = [sem(f"s_w_loaded{i}") for i in range(2)]
        s_up_ps = sem("s_up_ps")
        s_b1_cur = sem("s_b1_cur")
        s_hid = sem("s_hid")
        s_down_ps = sem("s_down_ps")
        s_fin_stats = sem("s_fin_stats")
        s_fin_mv = sem("s_fin_mv")
        s_fin_var = sem("s_fin_var")
        s_fin_rstd = sem("s_fin_rstd")
        s_fin = sem("s_fin")
        s_out = sem("s_out")
        up_banks = (0, 1, 2, 3)
        down = [bank(4 + i).rearrange("p (t d) -> p t d", t=4) for i in range(2)]
        hid = [prob_t[:].rearrange("p g j s -> p g (j s)"), prob[:].rearrange("p (g j) s -> p g (j s)", g=G)]

        ROWS = B // 2
        CH = 2
        NCH = B // CH

        block = ctx.enter_context(nc.Block())

        @block.sync
        def _(sp):
            for half in range(2):
                r = slice(ROWS * half, ROWS * half + ROWS)
                sp.dma_start(x0[:, r, :], t["x"][r].rearrange("b s d -> s b d")).then_inc(s_x, 16)
            b_qkv = t["L0_attn_b_qkv"]
            col = lambda v: v.rearrange("(p a) -> p a", a=1)
            row = lambda v: v.rearrange("(a d) -> a d", a=1).broadcast_to([P, D])
            for i, v in enumerate((b_qkv[0:D], b_qkv[D:2 * D])):
                sp.dma_start(bias_cols[:, i:i + 1], col(v)).then_inc(s_small, 16)
            for i, v in enumerate((b_qkv[2 * D:], t["L0_attn_b_out"])):
                sp.dma_start(bias_rows[:, i, :], row(v)).then_inc(s_small, 16)
            sp.dma_start(w_out[:], t["L0_attn_w_out"]).then_inc(s_small, 16)
            for i, n in enumerate(("Wq", "Wk", "Wv", "Wo")):
                sp.dma_start(w_cross[:, i, :], t["L0_xattn_" + n]).then_inc(s_w_cross, 16)
            for i, v in enumerate((t["L0_xattn_bq"], t["L0_xattn_bk"])):
                sp.dma_start(bias_cols[:, 2 + i:3 + i], col(v)).then_inc(s_w_late, 16)
            for i, v in enumerate((t["L0_xattn_bv"], t["L0_xattn_bo"])):
                sp.dma_start(bias_rows[:, 2 + i, :], row(v)).then_inc(s_w_late, 16)
            sp.dma_start(b1_rows[:], t["L0_ffn_b1"].rearrange("e (c p) -> (e c) p", p=P)).then_inc(s_w_late, 16)
            sp.dma_start(b2_rows[:], t["L0_ffn_b2"]).then_inc(s_w_late, 16)
            sp.dma_start(gate_w[:], t["L0_ffn_gate_w"]).then_inc(s_w_late, 16)

            def load_expert(e, slot):
                sp.dma_start(w1[:, slot, :], t["L0_ffn_w1"][bass.ds(e, 1)].rearrange("e d f -> d (e f)")).then_inc(s_w_loaded[slot], 16)
                sp.dma_start(w2[:, slot, :, :], t["L0_ffn_w2"][bass.ds(e, 1)].rearrange("e (c p) d -> p (e c) d", p=P)).then_inc(s_w_loaded[slot], 16)

            load_expert(0, 0)
            load_expert(1, 1)
            with sp.Fori(1, E // 2) as p:
                for slot in range(2):
                    sp.wait_ge(s_down_ps, 4 * p + 2 * slot - 2)
                    load_expert(2 * p + slot, slot)
            for half in range(2):
                sp.wait_ge(s_fin, half + 1)
                r = slice(ROWS * half, ROWS * half + ROWS)
                sp.dma_start(out[r].rearrange("b s d -> s b d"), acc[:, r, :]).then_inc(s_out, 16)
            sp.wait_ge(s_out, 32)

        @block.gpsimd
        def _(pool):
            g = nc.gpsimd
            copy = lambda o, i: g.tensor_scalar(o, i, 1.0, 1.0, ALU.mult, ALU.mult)
            g.memset(ones[:], 1.0).then_inc(s_ones, 1)
            g.memset(band4[:], 0.0).then_inc(s_band_zero, 1)
            g.memset(neg_half[:], -0.5).then_inc(s_neg_half, 1)
            g.iota(rank_i[:], pattern=[[-1, E]], base=E, channel_multiplier=0).then_inc(s_rank_i, 1)
            pool.wait_ge(s_ones, 1)
            g.affine_select(out=ident[:], in_=ones[:], compare_op=ALU.is_equal, fill=0.0, base=0,
                            pattern=[[-1, P]], channel_multiplier=1).then_inc(s_ident, 1)
            pool.wait_ge(s_band_zero, 1)
            g.affine_select(out=band4[:], in_=band4[:], compare_op=ALU.is_ge, fill=MASKED, base=BAND,
                            pattern=[[0, J], [1, S]], channel_multiplier=-1).then_inc(s_band_half, 1)
            pool.wait_ge(s_band_half, 1)
            g.affine_select(out=band4[:], in_=band4[:], compare_op=ALU.is_ge, fill=MASKED, base=BAND,
                            pattern=[[0, J], [-1, S]], channel_multiplier=1).then_inc(s_band, 1)
            pool.wait_ge(s_rank_i, 1)
            g.tensor_copy(rank[:], rank_i[:]).then_inc(s_rank, 1)

            def spread_keys(c, b, slot):
                for j in range(J):
                    last = g.tensor_scalar(c.kx[:, slot, :, j, :], c.ks[:, :, b, 0:c.n_keys],
                                           head_mask[:, j:j + 1], 1.0, ALU.mult, ALU.mult)
                last.then_inc(c.s_kx, 1)

            def rows(c):
                pool.wait_ge(c.s_rep_act, 8)
                pool.wait_ge(c.s_rep_dve, 8)
                pool.wait_ge(c.s_v_all, 2)
                def row_values(b):
                    if b >= 2:
                        pool.wait_ge(c.s_av_ps, 2 * b - 2)
                    copy(c.v[:, b % 2, :, 0:HD], c.v_all[:, b, :].rearrange("p (h d) -> p h d", d=HD)).then_inc(c.s_v, 1)

                for b in range(B):
                    if b >= 2:
                        pool.wait_ge(c.s_scores, 2 * b - 2)
                    spread_keys(c, b, b % 2)
                    copy(c.qs[:, b % 2], qs_all[:, :, b, :]).then_inc(c.s_qs, 1)
                    if b >= 1:
                        row_values(b - 1)
                row_values(B - 1)

            def residual(c):
                g.tensor_tensor(x_bo[:], c.x[:], bias_rows[:, c.bias_at + 1, :].unsqueeze(1).broadcast_to([S, B, D]), ALU.add).then_inc(c.s_x_bo, 1)

            def power(c):
                for half in range(2):
                    r = slice(ROWS * half, ROWS * half + ROWS)
                    pool.wait_ge(c.s_var_eps, half + 1)
                    g.tensor_tensor(rstd[:, r], var_eps[:, r], neg_half[:], ALU.pow).then_inc(c.s_rstd, 1)

            pool.wait_ge(s_head_mask, 1)
            pool.wait_ge(s_ones_col, 1)
            rows(self_)
            pool.wait_ge(s_small, 16 * 5)
            residual(self_)
            power(self_)
            pool.wait_ge(self_.s_normed, 2)
            pool.wait_ge(s_w_late, 16 * 7)
            rows(cross)
            residual(cross)
            power(cross)
            for half in range(2):
                r = slice(ROWS * half, ROWS * half + ROWS)
                pool.wait_ge(s_fin_var, half + 1)
                g.tensor_tensor(rstd[:, r], var_eps[:, r], neg_half[:], ALU.pow).then_inc(s_fin_rstd, 1)

        @block.tensor
        def _(pe):
            mm, tr = nc.tensor.matmul, nc.tensor.transpose

            def features_first(x, to_banks, s):
                for b in range(B):
                    last = tr(bank(to_banks[b // ROWS])[:, (b % ROWS) * S:(b % ROWS + 1) * S], x[:, b, :], ident[:])
                    if b % ROWS == ROWS - 1:
                        last.then_inc(s, 1)

            def project(w, x_t, width, banks, s):
                for half in range(2):
                    mm(bank(banks[half])[:, 0:ROWS * width], w, x_t[:, ROWS * half:ROWS * half + ROWS, :].rearrange("p b s -> p (b s)"),
                       start=True, stop=True).then_inc(s, 1)

            def project_values(c, banks):
                for b in range(B):
                    last = mm(bank(banks[b // ROWS])[0:c.n_keys, (b % ROWS) * D:(b % ROWS + 1) * D], c.kv_t[:, b, 0:c.n_keys], c.w[2],
                              start=True, stop=True)
                    if b % ROWS == ROWS - 1:
                        last.then_inc(c.s_v_ps, 1)

            def operands(c):
                n = 0
                for parts, names, width in ((q_parts, ("q1", "q2"), S), (k_parts, ("k1", "k2"), c.kp)):
                    for half in range(2):
                        for g in range(G):
                            if n >= 8:
                                pe.wait_ge(c.s_rep_dve if n % 2 else c.s_rep_act, (n - 8) // 2 + 1)
                            o = bank(n % 8)[:, 0:ROWS * width]
                            for i in range(2):
                                last = mm(o, sel[names[i]][:, g, :, :].rearrange("p t r -> p (t r)"),
                                          parts[i][:, ROWS * half * width:ROWS * (half + 1) * width], start=i == 0, stop=i == 1)
                            last.then_inc(c.s_rep_ps, 1)
                            n += 1

            def scores(c, b, half, slot):
                if half == 0:
                    pe.wait_ge(c.s_qs, b + 1)
                    pe.wait_ge(c.s_kx, b + 1)
                for n in range(2):
                    g = 2 * half + n
                    o = bank(g)[:, 0:J * c.n_keys]
                    last = mm(o, c.qs[:, slot, g, :], c.kx[:, slot, g, :, :].rearrange("p j k -> p (j k)"), start=True, stop=not c.masked)
                    if c.masked:
                        last = mm(o, ident_bf[:], band4[:].rearrange("p j k -> p (j k)"), start=False, stop=True)
                last.then_inc(c.s_scores, 1)

            def transposed(c, b, half, n):
                g = 2 * half + n
                for j in range(J):
                    last = tr(bank(PT + n)[0:c.n_keys, j * S:(j + 1) * S], c.prob[:, g * J + j, :], ident[:])
                last.then_inc(c.s_prob_t_ps, 1)

            def values(c, b, half, slot, n):
                g = 2 * half + n
                pe.wait_ge(c.s_prob_t, 4 * b + g + 1)
                for j in range(J):
                    last = mm(bank(AV + slot)[32 * j:32 * j + 32, g * S:(g + 1) * S], c.v[:, slot, g * J + j, :], c.prob_t[:, g, j, :],
                              start=True, stop=True, tile_position=(0, 32 * j))
                if n == 1:
                    last.then_inc(c.s_av_ps, 1)

            def rows(c):
                def row(b, slot, first=False, following=True):
                    for half in range(2):
                        if following:
                            pe.wait_ge(c.s_shifted, 2 * b + half + 1)
                            scores(c, b + 1, half, 1 - slot)
                        pe.wait_ge(c.s_prob, 2 * b + half + 1)
                        if half == 1:
                            pe.wait_ge(c.s_v, b + 1)
                        for n in range(2):
                            if half == 1 or not first:
                                pe.wait_ge(c.s_prob_t, 4 * b + 2 * half + n - 1)
                            transposed(c, b, half, n)
                            if half == 1:
                                values(c, b, 0, slot, n)
                            elif not first:
                                values(c, b - 1, 1, 1 - slot, n)

                if c.masked:
                    pe.wait_ge(s_band, 1)
                scores(c, 0, 0, 0)
                scores(c, 0, 1, 0)
                row(0, 0, first=True)
                with pe.Fori(0, B // 2 - 1) as p:
                    row(2 * p + 1, 1)
                    row(2 * p + 2, 0)
                row(B - 1, 1, following=False)
                for n in range(2):
                    values(c, B - 1, 1, 1, n)

            def output(c):
                for k in range(NCH):
                    for b in range(CH * k, CH * k + CH):
                        pe.wait_ge(c.s_av, b + 1)
                        if k >= 2 and b % CH == 0:
                            pe.wait_ge(c.s_att, k - 1)
                        for g in range(G):
                            last = tr(bank(b % 4)[:, g * S:(g + 1) * S], av_all[:, b, g * S:(g + 1) * S], ident[:])
                    last.then_inc(c.s_back, 1)
                    if k >= 1:
                        project_out(c, k - 1)
                project_out(c, NCH - 1)

            def project_out(c, k):
                pe.wait_ge(c.s_att, k + 1)
                if k == 0:
                    pe.wait_ge(c.s_prob_t, 4 * B)
                for b in range(CH * k, CH * k + CH):
                    last = tr(bank(4)[:, (b % CH) * S:(b % CH + 1) * S], att[:, b, :], ident[:])
                last.then_inc(c.s_att_t_ps, 1)
                pe.wait_ge(c.s_att_t, k + 1)
                for b in range(CH * k, CH * k + CH):
                    last = mm(bank(6 + b // ROWS)[:, (b % ROWS) * D:(b % ROWS + 1) * D], att_t[:, b, :], c.w[3], start=True, stop=True)
                if k % 2:
                    last.then_inc(c.s_out_ps, 1)

            pe.wait_ge(s_ident, 1)
            pe.wait_ge(s_x, 32)
            features_first(x0, (0, 1), self_.s_xt_ps)
            pe.wait_ge(self_.s_xt, 2)
            pe.wait_ge(s_w_qkv, 16)
            project(self_.w[0], xt, S, (2, 3), self_.s_q_ps)
            project(self_.w[1], xt, S, (4, 5), self_.s_k_ps)
            project_values(self_, (6, 7))
            pe.wait_ge(s_context, 16)
            for b in range(B):
                last = tr(bank(b // ROWS)[:, (b % ROWS) * SKP:(b % ROWS) * SKP + SK], context[:, b, :], ident[0:SK, 0:SK])
            last.then_inc(s_context_t_ps, 1)
            pe.wait_ge(self_.s_q_part2, 2)
            pe.wait_ge(s_w_cross, 64)
            pe.wait_ge(s_w_late, 16 * 7)
            for i in range(4):
                tr(bank(2)[:, i * D:(i + 1) * D], w_cross[:, i, :], ident[:])
            tr(bank(3)[:, 0:E * FC], b1_rows[:], ident[0:E * FC, 0:E * FC]).then_inc(s_wt_ps, 1)
            pe.wait_ge(s_sel, 4)
            pe.wait_ge(s_context_t, 1)
            pe.wait_ge(s_b1_sb, 1)
            pe.wait_ge(self_.s_k_part2, 2)
            pe.wait_ge(self_.s_v_all, 2)
            operands(self_)
            rows(self_)
            output(self_)
            pe.wait_ge(s_wt_sb, 1)
            project(cross.w[1], context_t, SKP, (0, 1), cross.s_k_ps)
            project_values(cross, (2, 3))
            pe.wait_ge(self_.s_normed, 2)
            features_first(x1, (4, 5), cross.s_xt_ps)
            pe.wait_ge(cross.s_xt, 2)
            project(cross.w[0], xt, S, (6, 7), cross.s_q_ps)
            pe.wait_ge(cross.s_v_all, 2)
            pe.wait_ge(cross.s_k_part2, 2)
            pe.wait_ge(cross.s_q_part2, 2)
            operands(cross)
            rows(cross)
            output(cross)
            pe.wait_ge(cross.s_normed, 2)
            features_first(x2, (0, 1), s_x2_t_ps)

            pe.wait_ge(s_x2_t, 2)
            for b in range(B):
                last = mm(bank(2)[:, b * E:(b + 1) * E], x2_t[:, b, :], gate_w[:], start=True, stop=True)
            last.then_inc(s_logits_ps, 1)
            pe.wait_ge(s_gates, 1)
            for b in range(B):
                last = tr(bank(6 + b // ROWS)[0:E, (b % ROWS) * P:(b % ROWS + 1) * P], gates[:, b, :], ident[:])
            last.then_inc(s_gates_t_ps, 1)
            pe.wait_ge(s_gates_t_sb, 1)
            for b in range(B):
                last = mm(down[b // ROWS][:, b % ROWS, :], gates_t[:, b, :], b2_rows[:], start=True, stop=True)
            last.then_inc(s_b2_ps, 1)
            pe.wait_ge(s_acc, 1)
            with pe.Fori(0, E // 2) as p:
                for slot in range(2):
                    e = 2 * p + slot
                    pe.wait_ge(s_w_loaded[slot], 32 * p + 32)
                    for half in range(2):
                        for c in range(FC):
                            pe.wait_ge(s_hid, 8 * e + half * FC + c + 1)
                            mm(bank(up_banks[c]), w1[:, slot, c * P:(c + 1) * P],
                               x2_t[:, ROWS * half:ROWS * half + ROWS, :].rearrange("p b s -> p (b s)"), start=True, stop=True).then_inc(s_up_ps, 1)
                    for half in range(2):
                        pe.wait_ge(s_hid, 8 * e + 4 * half + 8)
                        pe.wait_ge(s_acc, 2 * e + half + 1)
                        for tt in range(ROWS):
                            for c in range(FC):
                                last = mm(down[half][:, tt, :], hid[half][:, c, tt * P:(tt + 1) * P], w2[:, slot, c, :],
                                          start=c == 0, stop=c == FC - 1)
                        last.then_inc(s_down_ps, 1)

        @block.scalar
        def _(act):
            copy = lambda o, i: nc.scalar.activation(o, i, ACT.Copy)
            act.dma_start(w_qkv[:], t["L0_attn_w_qkv"]).then_inc(s_w_qkv, 16)
            act.dma_start(context[:], t["ctx_1024"].rearrange("b s d -> s b d")).then_inc(s_context, 16)

            def first_parts(s_ps, banks, parts, width, bias, s):
                for half in range(2):
                    act.wait_ge(s_ps, half + 1)
                    nc.scalar.activation(parts[0][:, ROWS * width * half:ROWS * width * (half + 1)], bank(banks[half])[:, 0:ROWS * width],
                                         ACT.Identity, bias=bias_cols[:, bias:bias + 1]).then_inc(s, 1)

            def operands(c):
                for n in range(0, 16, 2):
                    to, width = (qs_all, S) if n < 8 else (ks_all, c.kp)
                    half, g = n % 8 // 4, n % 4
                    act.wait_ge(c.s_rep_ps, n + 1)
                    copy(to[:, g, ROWS * half:ROWS * half + ROWS, 0:width],
                         bank(n % 8)[:, 0:ROWS * width].rearrange("p (b s) -> p b s", b=ROWS)).then_inc(c.s_rep_act, 1)

            def rows(c):
                def exps(b, half):
                    act.wait_ge(c.s_shifted, 2 * b + half + 1)
                    o = c.prob[:, 8 * half:8 * half + 8, :].rearrange("p h k -> p (h k)")
                    nc.scalar.activation(o, o, ACT.Exp, scale=c.scale).then_inc(c.s_prob, 1)

                def evacuate(b, half):
                    for n in range(2):
                        g = 2 * half + n
                        act.wait_ge(c.s_prob_t_ps, 4 * b + g + 1)
                        copy(c.prob_t[:, g, :, :].rearrange("p j s -> p (j s)"), bank(PT + n)[0:c.n_keys, :]).then_inc(c.s_prob_t, 1)

                def read_values(b, slot):
                    act.wait_ge(c.s_av_ps, 2 * b + 2)
                    copy(av_all[:, bass.ds(b, 1), :], bank(AV + slot).rearrange("p (a n) -> p a n", a=1)).then_inc(c.s_av, 1)

                def row(b, slot):
                    exps(b, 0)
                    evacuate(b - 1, 1)
                    exps(b, 1)
                    evacuate(b, 0)
                    read_values(b - 1, 1 - slot)

                exps(0, 0)
                exps(0, 1)
                evacuate(0, 0)
                with act.Fori(0, B // 2 - 1) as p:
                    row(2 * p + 1, 1)
                    row(2 * p + 2, 0)
                row(B - 1, 1)
                evacuate(B - 1, 1)
                read_values(B - 1, 1)

            def output(c):
                for k in range(NCH):
                    act.wait_ge(c.s_att_t_ps, k + 1)
                    copy(att_t[:, CH * k:CH * k + CH, :].rearrange("p b s -> p (b s)"), bank(4)[:, 0:CH * S]).then_inc(c.s_att_t, 1)

            def features_first(to, b, s_ps, s):
                act.wait_ge(s_ps, 1)
                copy(to[:, 0:ROWS, :].rearrange("p b s -> p (b s)"), bank(b)).then_inc(s, 1)

            act.wait_ge(s_ident, 1)
            copy(ident_bf[:], ident[:]).then_inc(s_ident_bf, 1)
            features_first(xt, 0, self_.s_xt_ps, self_.s_xt)
            act.wait_ge(s_small, 16 * 5)
            first_parts(self_.s_q_ps, (2, 3), q_parts, S, 0, self_.s_q_part1)
            first_parts(self_.s_k_ps, (4, 5), k_parts, S, 1, self_.s_k_part1)
            act.wait_ge(s_context_t_ps, 1)
            for half in range(2):
                last = copy(context_t[:, ROWS * half:ROWS * half + ROWS, 0:SK],
                            bank(half)[:, 0:ROWS * SKP].rearrange("p (b s) -> p b s", s=SKP)[:, :, 0:SK])
            last.then_inc(s_context_t, 1)
            act.wait_ge(s_wt_ps, 1)
            copy(w_cross_t[:].rearrange("p a d -> p (a d)"), bank(2)).then_inc(s_wt_sb, 1)
            copy(b1_t[:], bank(3)[:, 0:E * FC]).then_inc(s_b1_sb, 1)
            operands(self_)
            rows(self_)
            output(self_)
            first_parts(cross.s_k_ps, (0, 1), k_parts, SKP, 3, cross.s_k_part1)
            features_first(xt, 4, cross.s_xt_ps, cross.s_xt)
            first_parts(cross.s_q_ps, (6, 7), q_parts, S, 2, cross.s_q_part1)
            operands(cross)
            rows(cross)
            output(cross)
            features_first(x2_t, 0, s_x2_t_ps, s_x2_t)

            act.wait_ge(s_route, 2)
            nc.scalar.activation(rt[1][:], rt[0][:], ACT.Exp).then_inc(s_route_e, 1)
            act.wait_ge(s_gates_t_ps, 1)
            for half in range(2):
                last = copy(gates_t[:, ROWS * half:ROWS * half + ROWS, :].rearrange("p b s -> p (b s)"), bank(6 + half)[0:E, :])
            last.then_inc(s_gates_t_sb, 1)
            with act.Fori(0, E) as e:
                act.wait_ge(s_b1_cur, e + 1)
                for half in range(2):
                    for c in range(FC):
                        act.wait_ge(s_up_ps, 8 * e + 4 * half + c + 1)
                        nc.scalar.activation(hid[half][:, c, :], bank(up_banks[c]), ACT.Gelu, bias=b1_cur[:, c:c + 1]).then_inc(s_hid, 1)

        @block.vector
        def _(dve):
            v = nc.vector

            def second_parts(s_part1, banks, parts, width, bias, s):
                for half in range(2):
                    o = slice(ROWS * width * half, ROWS * width * (half + 1))
                    dve.wait_ge(s_part1, half + 1)
                    v.scalar_tensor_tensor(parts[1][:, o], bank(banks[half])[:, 0:ROWS * width], bias_cols[:, bias:bias + 1],
                                           parts[0][:, o].bitcast(F32), ALU.add, ALU.subtract).then_inc(s, 1)

            def values(c, banks):
                n = c.n_keys
                for half in range(2):
                    dve.wait_ge(c.s_v_ps, half + 1)
                    v.tensor_tensor(c.v_all[:, ROWS * half:ROWS * half + ROWS, :], bank(banks[half])[0:n, :].rearrange("p (b d) -> p b d", b=ROWS),
                                    bias_rows[0:n, c.bias_at, :].unsqueeze(1).broadcast_to([n, ROWS, D]), ALU.add).then_inc(c.s_v_all, 1)

            def operands(c):
                for n in range(1, 16, 2):
                    to, width = (qs_all, S) if n < 8 else (ks_all, c.kp)
                    half, g = n % 8 // 4, n % 4
                    dve.wait_ge(c.s_rep_ps, n + 1)
                    v.tensor_copy(to[:, g, ROWS * half:ROWS * half + ROWS, 0:width],
                                  bank(n % 8)[:, 0:ROWS * width].rearrange("p (b s) -> p b s", b=ROWS)).then_inc(c.s_rep_dve, 1)

            def rows(c):
                def half_row(b, half, first=False):
                    dve.wait_ge(c.s_scores, 2 * b + half + 1)
                    sc = ps[:, 2 * half:2 * half + 2, 0:J * c.n_keys].rearrange("p g (j k) -> p g j k", j=J)
                    m = mx[:, 8 * half:8 * half + 8].rearrange("p (g j) -> p g j", j=J)
                    v.tensor_reduce(m, sc, AX.X, ALU.max).then_inc(c.s_mx, 1)
                    dve.wait_ge(c.s_mx, 2 * b + half + 1)
                    if not first:
                        dve.wait_ge(c.s_prob_t_ps, 4 * b + 2 * half - 2)
                    o = c.prob[:, 8 * half:8 * half + 8, :].rearrange("p (g j) k -> p g j k", j=J)
                    v.tensor_tensor(o, sc, m.unsqueeze(3).broadcast_to([S, 2, J, c.n_keys]), ALU.subtract).then_inc(c.s_shifted, 1)

                for half in range(2):
                    half_row(0, half, first=True)
                with dve.Fori(1, B) as b:
                    for half in range(2):
                        half_row(b, half)

            def normalise(c):
                for k in range(NCH):
                    dve.wait_ge(c.s_back, k + 1)
                    r = slice(CH * k, CH * k + CH)
                    first = CH * k % 4
                    back = ps[:, first:first + CH, :].rearrange("p b (h w) -> p b h w", w=32)
                    v.reciprocal(rden[:, r, :].unsqueeze(3), back[:, :, :, HD:HD + 1]).then_inc(c.s_rden, 1)
                    dve.wait_ge(c.s_rden, k + 1)
                    v.tensor_tensor(att[:, r, :].rearrange("p b (h d) -> p b h d", d=HD), back[:, :, :, 0:HD],
                                    rden[:, r, :].unsqueeze(3).broadcast_to([S, CH, H, HD]), ALU.mult).then_inc(c.s_att, 1)

            def output(c):
                normalise(c)
                dve.wait_ge(c.s_x_bo, 1)
                for half in range(2):
                    r = slice(ROWS * half, ROWS * half + ROWS)
                    dve.wait_ge(c.s_out_ps, half + 1)
                    v.tensor_tensor(res[:, r, :], bank(6 + half).rearrange("p (b d) -> p b d", b=ROWS), x_bo[:, r, :], ALU.add).then_inc(c.s_res, 1)
                    dve.wait_ge(c.s_res, half + 1)
                    layer_stats(res, half, c.s_stats, c.s_mv, c.s_var_eps)
                for half in range(2):
                    dve.wait_ge(c.s_rstd, half + 1)
                    layer_norm(c.to, res, half, c.s_normed)

            def layer_stats(a, half, s_stats, s_mv, s_var_eps):
                rs_ = range(ROWS * half, ROWS * half + ROWS)
                for b in rs_:
                    last = v.bn_stats(stats[:, b, :], a[:, b, :])
                last.then_inc(s_stats, 1)
                dve.wait_ge(s_stats, half + 1)
                for b in rs_:
                    last = v.bn_aggr(mv[:, b, :], stats[:, b, :])
                last.then_inc(s_mv, 1)
                dve.wait_ge(s_mv, half + 1)
                r = slice(ROWS * half, ROWS * half + ROWS)
                v.tensor_scalar(var_eps[:, r].unsqueeze(2), mv[:, r, 1:2], EPS, None, ALU.add).then_inc(s_var_eps, 1)

            def layer_norm(to, a, half, s):
                for b in range(ROWS * half, ROWS * half + ROWS):
                    last = v.tensor_scalar(to[:, b, :], a[:, b, :], mv[:, b, 0:1], rstd[:, b:b + 1], ALU.subtract, ALU.mult)
                last.then_inc(s, 1)

            def features_first(to, b, s_ps, s):
                dve.wait_ge(s_ps, 2)
                v.tensor_copy(to[:, ROWS:B, :].rearrange("p b s -> p (b s)"), bank(b)).then_inc(s, 1)

            v.memset(v_row[:], 0.0).then_inc(s_zeroed, 1)
            v.memset(context_t[:, :, SK:], 0.0).then_inc(s_zeroed, 1)
            for n in sel_names:
                v.memset(sel[n][:].bitcast(F32), 0.0).then_inc(s_zeroed, 1)
            dve.wait_ge(s_zeroed, 6)
            v.memset(v_row[:, :, :, HD:HD + 1], 1.0).then_inc(s_ones_col, 1)
            dve.wait_ge(s_ident, 1)
            by_group = ident[:].rearrange("p (g r) -> p g r", r=R)
            for n, quadrants in zip(sel_names, ((0, 1), (2, 3), (0, 2), (1, 3))):
                for q in quadrants:
                    last = v.tensor_copy(sel[n][:, :, q, :], by_group)
                last.then_inc(s_sel, 1)
            v.tensor_reduce(head_mask[:], ident[:].rearrange("p (q j d) -> p j q d", q=4, d=HD), AX.XY, ALU.add).then_inc(s_head_mask, 1)

            features_first(xt, 1, self_.s_xt_ps, self_.s_xt)
            dve.wait_ge(s_small, 16 * 5)
            second_parts(self_.s_q_part1, (2, 3), q_parts, S, 0, self_.s_q_part2)
            second_parts(self_.s_k_part1, (4, 5), k_parts, S, 1, self_.s_k_part2)
            values(self_, (6, 7))
            operands(self_)
            rows(self_)
            output(self_)
            dve.wait_ge(s_w_late, 16 * 7)
            second_parts(cross.s_k_part1, (0, 1), k_parts, SKP, 3, cross.s_k_part2)
            values(cross, (2, 3))
            features_first(xt, 5, cross.s_xt_ps, cross.s_xt)
            second_parts(cross.s_q_part1, (6, 7), q_parts, S, 2, cross.s_q_part2)
            operands(cross)
            rows(cross)
            output(cross)
            features_first(x2_t, 1, s_x2_t_ps, s_x2_t)

            per_token = lambda a: a[:].unsqueeze(2).broadcast_to([P, B, E])
            dve.wait_ge(s_logits_ps, 1)
            v.tensor_copy(logits[:].rearrange("p b e -> p (b e)"), bank(2)[:, 0:B * E]).then_inc(s_route, 1)
            for c in range(FC):
                v.memset(b1_cur[:, c:c + 1], 0.0).then_inc(s_hid, 1)
            dve.wait_ge(s_route, 1)
            v.tensor_reduce(rs[0][:], logits[:], AX.X, ALU.max).then_inc(s_route_e, 1)
            dve.wait_ge(s_route_e, 1)
            v.tensor_tensor(rt[0][:], logits[:], per_token(rs[0]), ALU.subtract).then_inc(s_route, 1)
            dve.wait_ge(s_route, 2)
            v.tensor_scalar(rt[2][:], rt[0][:], 0.0, None, ALU.is_equal).then_inc(s_route, 1)
            dve.wait_ge(s_route_e, 2)
            v.tensor_reduce(rs[1][:], rt[1][:], AX.X, ALU.add).then_inc(s_route, 1)
            dve.wait_ge(s_route, 4)
            v.reciprocal(rs[2][:], rs[1][:]).then_inc(s_route, 1)
            dve.wait_ge(s_rank, 1)
            v.tensor_tensor(logits[:], rt[2][:], rank[:].unsqueeze(1).broadcast_to([P, B, E]), ALU.mult).then_inc(s_route, 1)
            dve.wait_ge(s_route, 6)
            v.tensor_reduce(rs[0][:], logits[:], AX.X, ALU.max).then_inc(s_route, 1)
            dve.wait_ge(s_route, 7)
            v.tensor_tensor(rt[1][:], logits[:], per_token(rs[0]), ALU.is_equal).then_inc(s_route, 1)
            dve.wait_ge(s_route, 8)
            v.tensor_tensor(gates[:], rt[1][:], per_token(rs[2]), ALU.mult).then_inc(s_gates, 1)
            dve.wait_ge(s_b2_ps, 1)
            for half in range(2):
                r = slice(ROWS * half, ROWS * half + ROWS)
                v.tensor_tensor(acc[:, r, :], down[half], x2[:, r, :], ALU.add).then_inc(s_acc, 1)
            with dve.Fori(0, E) as e:
                dve.wait_ge(s_hid, 8 * e + 4)
                v.tensor_copy(b1_cur[:], b1_t[:, bass.ds(e * FC, FC)]).then_inc(s_b1_cur, 1)
                for half in range(2):
                    dve.wait_ge(s_down_ps, 2 * e + half + 1)
                    dve.wait_ge(s_acc, 2 * e + half + 1)
                    for tt in range(ROWS):
                        b = ROWS * half + tt
                        last = v.scalar_tensor_tensor(acc[:, b, :], down[half][:, tt, :], gates[:, b, bass.ds(e, 1)], acc[:, b, :], ALU.mult, ALU.add)
                    last.then_inc(s_acc, 1)
            dve.wait_ge(s_acc, 2 * E + 2)
            for half in range(2):
                layer_stats(acc, half, s_fin_stats, s_fin_mv, s_fin_var)
            for half in range(2):
                dve.wait_ge(s_fin_rstd, half + 1)
                layer_norm(acc, acc, half, s_fin)


_INS = ['x', 'ctx_1024', 'L0_attn_w_qkv', 'L0_attn_b_qkv', 'L0_attn_w_out', 'L0_attn_b_out', 'L0_xattn_Wq', 'L0_xattn_bq',
        'L0_xattn_Wk', 'L0_xattn_bk', 'L0_xattn_Wv', 'L0_xattn_bv', 'L0_xattn_Wo', 'L0_xattn_bo', 'L0_ffn_gate_w',
        'L0_ffn_w1', 'L0_ffn_b1', 'L0_ffn_w2', 'L0_ffn_b2']


def kernel(**inputs):
    import numpy as _np
    import concourse.bacc as _bacc
    from concourse import mybir as _mybir
    from concourse.bass_utils import run_bass_kernel_spmd as _run

    nc = _bacc.Bacc("TRN2", target_bir_lowering=False, num_devices=1)
    arrays, aps = {}, {}
    for name in _INS:
        a = _np.ascontiguousarray(inputs[name])
        arrays[f"in_{name}"] = a
        aps[name] = nc.dram_tensor(f"in_{name}", a.shape, _mybir.dt.from_np(a.dtype), kind="ExternalInput").ap()
    out = nc.dram_tensor("out_0", (B, S, D), F32, kind="ExternalOutput").ap()
    build(nc, aps, out)
    r = _run(nc, [arrays], core_ids=[0])
    return r.results[0]["out_0"]
```

```python
from contextlib import ExitStack

import concourse.bass as bass
from concourse import mybir

F32 = mybir.dt.float32
F32R = mybir.dt.float32r
I32 = mybir.dt.int32
U32 = mybir.dt.uint32
BF16 = mybir.dt.bfloat16
ACT = mybir.ActivationFunctionType
ALU = mybir.AluOpType
AX = mybir.AxisListType

P = 128
B, S, D = 8, 128, 128
H, HD = 16, 8
G, J = 4, 4
R = J * HD
SK = 77
SKP = 80
BAND = 32
E, FF = 8, 512
FC = FF // P
EPS = 1e-5
MASKED = -1e30
NB = B * S // P + E - 1
GATE, TOKEN = D, D + 1
RW = D + 2
NO_TOKEN = B * S


class Chain:
    pass


def build(nc, t, out, slots):
    with ExitStack() as ctx:
        def sb(name, shape, dt=F32):
            return ctx.enter_context(nc.sbuf_tensor(name, shape, dt))

        def sem(name):
            return ctx.enter_context(nc.semaphore(name))

        ps = ctx.enter_context(nc.psum_tensor("ps", [P, 8, 512], F32))
        bank = lambda i: ps[:, i, :]
        PT, AV = 4, 6

        ident = sb("ident", [P, P])
        ident_bf = sb("ident_bf", [P, P], BF16)
        ones = sb("ones", [P, P])
        band4 = sb("band4", [P, J, S], BF16)
        ones_bf = sb("ones_bf", [P, P], BF16)
        before = sb("before", [P, P], BF16)
        sizes_i = sb("sizes_i", [P, B], I32)
        sizes = sb("sizes", [P, B])
        blocks_i = sb("blocks_i", [P, 16], I32)
        blocks = sb("blocks", [P, 16])
        slots_below = sb("slots_below", [P, E, E])
        sel_names = ("q1", "q2", "k1", "k2")
        sel = {n: sb("sel_" + n, [P, G, 4, R], F32R) for n in sel_names}
        head_mask = sb("head_mask", [P, J])
        neg_half = sb("neg_half", [P, 4])
        s_ones = sem("s_ones")
        s_ident = sem("s_ident")
        s_band_zero = sem("s_band_zero")
        s_band_half = sem("s_band_half")
        s_band = sem("s_band")
        s_neg_half = sem("s_neg_half")
        s_ident_bf = sem("s_ident_bf")
        s_sort_half = sem("s_sort_half")
        s_sort = sem("s_sort")
        s_pad = sem("s_pad")
        s_prefilled = sem("s_prefilled")
        s_zeroed = sem("s_zeroed")
        s_sel = sem("s_sel")
        s_ones_col = sem("s_ones_col")
        s_head_mask = sem("s_head_mask")

        w_qkv = sb("w_qkv", [D, 3 * D])
        w_out = sb("w_out", [D, D])
        w_cross = sb("w_cross", [D, 4, D])
        w_cross_t = sb("w_cross_t", [D, 4, D])
        bias_cols = sb("bias_cols", [P, 4])
        bias_rows = sb("bias_rows", [P, 4, D])
        b1_rows = sb("b1_rows", [E * FC, P])
        b1_t = sb("b1_t", [P, E * FC])
        b2_all = sb("b2_all", [P, E, D])
        gate_w = sb("gate_w", [D, E])
        w1_cur = sb("w1_cur", [D, 2, FF])
        b1_cur = sb("b1_cur", [P, 2, FC])
        s_w_qkv = sem("s_w_qkv")
        s_small = sem("s_small")
        s_w_cross = sem("s_w_cross")
        s_w_late = sem("s_w_late")
        s_wt_ps = sem("s_wt_ps")
        s_wt_sb = sem("s_wt_sb")
        s_b1_sb = sem("s_b1_sb")

        parts_all = sb("parts_all", [P, 4, B * S], F32R)
        q_parts = [parts_all[:, i, :] for i in (0, 1)]
        k_parts = [parts_all[:, i, :] for i in (2, 3)]
        qs_all = sb("qs_all", [P, G, B, S])
        ks_all = sb("ks_all", [P, G, B, S])
        av_all = sb("av_all", [P, B, G * S])
        prob = sb("prob", [S, H, S])
        prob_t = sb("prob_t", [S, G, J, S])
        qs = sb("qs", [P, 2, G, S], F32R)
        kx = sb("kx", [P, 2, G, J * S], F32R)
        v_row = sb("v_row", [P, 2, H, 32])
        mx = sb("mx", [S, H])
        rden = sb("rden", [S, B, H])
        att = sb("att", [S, B, D])
        att_t = sb("att_t", [D, B, S])
        stats = sb("stats", [S, B, 6])
        mv = sb("mv", [S, B, 2])
        var_eps = sb("var_eps", [S, B])
        rstd = sb("rstd", [S, B])

        def attention(name, n_keys, scale, masked, bias_at, x, xt, x_bo):
            c = Chain()
            c.n_keys, c.kp, c.scale, c.masked, c.bias_at = n_keys, n_keys + (-n_keys) % 16, scale, masked, bias_at
            c.x, c.xt, c.x_bo = x, xt, x_bo
            c.ks = ks_all[:, :, :, 0:c.kp]
            c.prob = prob[:].rearrange("p h k -> p (h k)")[:, 0:H * n_keys].rearrange("p (h k) -> p h k", h=H)
            c.prob_t = prob_t[0:n_keys]
            c.v_all = sb("v_all_" + name, [n_keys, B, D])
            c.qs = qs
            c.kx = kx[:].rearrange("p t g n -> p (t g n)")[:, 0:2 * H * n_keys].rearrange("p (t g j k) -> p t g j k", t=2, g=G, j=J)
            c.v = v_row[0:n_keys]
            c.s_xt_ps = sem(name + "_xt_ps")
            c.s_xt = [sem(f"{name}_xt{half}") for half in range(2)]
            c.s_x_bo = sem(name + "_x_bo")
            c.s_q_ps = sem(name + "_q_ps")
            c.s_q_part1 = sem(name + "_q_part1")
            c.s_q_part2 = sem(name + "_q_part2")
            c.s_k_ps = sem(name + "_k_ps")
            c.s_k_part1 = sem(name + "_k_part1")
            c.s_k_part2 = sem(name + "_k_part2")
            c.s_v_ps = sem(name + "_v_ps")
            c.s_v_all = sem(name + "_v_all")
            c.s_rep_ps = sem(name + "_rep_ps")
            c.s_rep_act = sem(name + "_rep_act")
            c.s_rep_dve = sem(name + "_rep_dve")
            c.s_qs = sem(name + "_qs")
            c.s_kx = sem(name + "_kx")
            c.s_v = sem(name + "_v")
            c.s_scores = sem(name + "_scores")
            c.s_mx = sem(name + "_mx")
            c.s_shifted = sem(name + "_shifted")
            c.s_prob = sem(name + "_prob")
            c.s_prob_t_ps = sem(name + "_prob_t_ps")
            c.s_prob_t = sem(name + "_prob_t")
            c.s_av_ps = sem(name + "_av_ps")
            c.s_av = sem(name + "_av")
            c.s_back = sem(name + "_back")
            c.s_rden = sem(name + "_rden")
            c.s_att = sem(name + "_att")
            c.s_att_t_ps = sem(name + "_att_t_ps")
            c.s_att_t = sem(name + "_att_t")
            c.s_out_ps = sem(name + "_out_ps")
            c.s_stats = sem(name + "_stats")
            c.s_mv = sem(name + "_mv")
            c.s_var_eps = sem(name + "_var_eps")
            c.s_rstd = sem(name + "_rstd")
            c.s_normed = sem(name + "_normed")
            return c

        x0 = sb("x0", [S, B, D])
        x1 = sb("x1", [S, B, D])
        x2_rows = sb("x2_rows", [S, B, RW])
        x2 = x2_rows[:, :, 0:D]
        xt = sb("xt", [D, B, S])
        x2_t = sb("x2_t", [D, B, S])
        x_bo = sb("x_bo", [S, B, D])
        self_ = attention("self", S, D ** -0.5, True, 0, x0, xt, x_bo)
        cross = attention("cross", SK, HD ** -0.5, False, 2, x1, xt, x_bo)
        context = sb("context", [SK, B, D])
        context_t = sb("context_t", [D, B, SKP])
        self_.kv_t, cross.kv_t = xt, context_t
        self_.w = (w_qkv[:, 0:D], w_qkv[:, D:2 * D], w_qkv[:, 2 * D:], w_out[:])
        cross.w = tuple(w_cross_t[:, i, :] for i in range(4))
        self_.to, cross.to = x1, x2
        self_.stages, self_.first_bank, self_.ready = ((False, 0), (True, 0), (False, 1), (True, 1)), 6, (8, 16)
        cross.stages, cross.first_bank, cross.ready = ((True, 0), (False, 0), (True, 1), (False, 1)), 0, (8, 16)
        s_x = sem("s_x")
        s_context = sem("s_context")
        s_context_t_ps = sem("s_context_t_ps")
        s_context_t = sem("s_context_t")
        s_x2_t_ps = sem("s_x2_t_ps")
        s_x2_t = [sem(f"s_x2_t{half}") for half in range(2)]

        shifted = sb("shifted", [P, B, E])
        exps = sb("exps", [P, B, E])
        ranked = sb("ranked", [P, B, E])
        top = sb("top", [P, B])
        top_rank = sb("top_rank", [P, B])
        sum_exps = sb("sum_exps", [P, B])
        rank = sb("rank", [P, E])
        rank_i = sb("rank_i", [P, E], I32)
        chosen = sb("chosen", [P, 2 * B, E], BF16)
        reaches = sb("reaches", [P, E, B])
        n_blocks = sb("n_blocks", [P, E])
        below = sb("below", [P, E, E])
        first_slot = sb("first_slot", [P, E])
        end_block = sb("end_block", [P, E])
        place = sb("place", [P, B, E])
        slot_of = sb("slot_of", [P, B], U32)
        ended = sb("ended", [1, 16, E])
        n_ended = sb("n_ended", [1, 16])
        expert_of = sb("expert_of", [1, 16], I32)
        w1_all = av_all[:].rearrange("p b n -> p (b n)").rearrange("p (e f) -> p e f", e=E)
        w2_all = ks_all[:].rearrange("p g b s -> p (g b s)").rearrange("p (e c d) -> p e c d", e=E, c=FC)
        qs_flat = qs_all[:].rearrange("p g b s -> p (g b s)")
        xin = qs_flat[:, 0:NB * RW].rearrange("p (j r) -> p j r", j=NB)
        normed = qs_flat[:, NB * RW:NB * (RW + D)].rearrange("p (j r) -> p j r", j=NB)
        xin_t = prob[:].rearrange("p h k -> p (h k)")[:, 0:NB * P].rearrange("p (j r) -> p j r", j=NB)
        hid = prob_t
        pad = sb("pad", [P, RW])
        gated = sb("gated", [P, 2, D])
        s_chosen = sem("s_chosen")
        s_rank_i = sem("s_rank_i")
        s_rank = sem("s_rank")
        s_logits_ps = sem("s_logits_ps")
        s_route = sem("s_route")
        s_exps = sem("s_exps")
        s_gate = sem("s_gate")
        s_token = sem("s_token")
        s_place_ps = sem("s_place_ps")
        s_slot_of = sem("s_slot_of")
        s_expert_of = sem("s_expert_of")
        s_w1_all = sem("s_w1_all")
        s_w2_all = sem("s_w2_all")
        s_sorted = sem("s_sorted")
        s_xin_t_ps = sem("s_xin_t_ps")
        s_cur = sem("s_cur")
        s_up_ps = sem("s_up_ps")
        s_hid = sem("s_hid")
        s_down_ps = sem("s_down_ps")
        s_plus_b2 = sem("s_plus_b2")
        s_gated = sem("s_gated")
        s_fin_stats = sem("s_fin_stats")
        s_fin_mv = sem("s_fin_mv")
        s_fin_var = sem("s_fin_var")
        s_fin_rstd = sem("s_fin_rstd")
        s_fin = sem("s_fin")
        s_out = sem("s_out")
        QUADS = [range(q, min(q + 4, NB)) for q in range(0, NB, 4)]
        LOADS = ((0, 4), (4, 12), (12, NB))
        s_xin = [sem(f"s_xin{i}") for i in range(len(LOADS))]
        s_xin_t = [sem(f"s_xin_t{q}") for q in range(len(QUADS))]

        ROWS = B // 2
        CH = 2
        NCH = B // CH

        def steps(c):
            for stage, (of_keys, half) in enumerate(c.stages):
                for g in range(G):
                    n = G * stage + g
                    yield n, of_keys, half, g, (n + (c.first_bank if n < 8 else 0)) % 8

        def operands_to_sb(c, engine, copy, odd, s, values=None):
            for n, of_keys, half, g, from_bank in steps(c):
                if n == 2 * G and values:
                    values()
                if n % 2 == odd:
                    to, width = (ks_all, c.kp) if of_keys else (qs_all, S)
                    engine.wait_ge(c.s_rep_ps, n + 1)
                    copy(to[:, g, ROWS * half:ROWS * half + ROWS, 0:width],
                         bank(from_bank)[:, 0:ROWS * width].rearrange("p (b s) -> p b s", b=ROWS)).then_inc(s, 1)

        quad_banks = (6, 7, 4, 5)

        def quad_to_sb(copy, q):
            first, n = QUADS[q][0], len(QUADS[q])
            copy(xin_t[:, first:first + n, :].rearrange("p j n -> p (j n)"), bank(quad_banks[q])[:, 0:n * P]).then_inc(s_xin_t[q], 1)

        block = ctx.enter_context(nc.Block())

        @block.sync
        def _(sp):
            for half in range(2):
                r = slice(ROWS * half, ROWS * half + ROWS)
                sp.dma_start(x0[:, r, :], t["x"][r].rearrange("b s d -> s b d")).then_inc(s_x, 16)
            b_qkv = t["L0_attn_b_qkv"]
            col = lambda v: v.rearrange("(p a) -> p a", a=1)
            row = lambda v: v.rearrange("(a d) -> a d", a=1).broadcast_to([P, D])
            for i, v in enumerate((b_qkv[0:D], b_qkv[D:2 * D])):
                sp.dma_start(bias_cols[:, i:i + 1], col(v)).then_inc(s_small, 16)
            for i, v in enumerate((b_qkv[2 * D:], t["L0_attn_b_out"])):
                sp.dma_start(bias_rows[:, i, :], row(v)).then_inc(s_small, 16)
            sp.dma_start(w_out[:], t["L0_attn_w_out"]).then_inc(s_small, 16)
            for i, n in enumerate(("Wq", "Wk", "Wv", "Wo")):
                sp.dma_start(w_cross[:, i, :], t["L0_xattn_" + n]).then_inc(s_w_cross, 16)
            for i, v in enumerate((t["L0_xattn_bq"], t["L0_xattn_bk"])):
                sp.dma_start(bias_cols[:, 2 + i:3 + i], col(v)).then_inc(s_w_late, 16)
            for i, v in enumerate((t["L0_xattn_bv"], t["L0_xattn_bo"])):
                sp.dma_start(bias_rows[:, 2 + i, :], row(v)).then_inc(s_w_late, 16)
            sp.dma_start(b1_rows[:], t["L0_ffn_b1"].rearrange("e (c p) -> (e c) p", p=P)).then_inc(s_w_late, 16)
            sp.dma_start(b2_all[:].rearrange("p e d -> p (e d)"),
                         t["L0_ffn_b2"].rearrange("(a e) d -> a (e d)", a=1).broadcast_to([P, E * D])).then_inc(s_w_late, 16)
            sp.dma_start(gate_w[:], t["L0_ffn_gate_w"]).then_inc(s_w_late, 16)

            sp.wait_ge(s_pad, 2)
            sp.dma_start(slots.rearrange("(j p) r -> p j r", p=P), pad[:].unsqueeze(1).broadcast_to([P, NB, RW])).then_inc(s_prefilled, 16)
            sp.wait_ge(cross.s_kx, B)
            sp.dma_start(w2_all, t["L0_ffn_w2"].rearrange("e (c p) d -> p e c d", p=P)).then_inc(s_w2_all, 16)
            sp.wait_ge(cross.s_back, NCH)
            sp.dma_start(w1_all, t["L0_ffn_w1"].rearrange("e d f -> d e f")).then_inc(s_w1_all, 16)
            sp.wait_ge(cross.s_qs, B)
            sp.wait_ge(s_sorted, 16 * B)
            by_block = slots.rearrange("(j p) r -> p j r", p=P)
            for s_load, (first, end) in zip(s_xin, LOADS):
                sp.dma_start(xin[:, first:end, :], by_block[:, first:end, :]).then_inc(s_load, 16)

        @block.gpsimd
        def _(pool):
            g = nc.gpsimd
            copy = lambda o, i: g.tensor_scalar(o, i, 1.0, 1.0, ALU.mult, ALU.mult)
            g.memset(ones[:], 1.0).then_inc(s_ones, 1)
            g.memset(band4[:], 0.0).then_inc(s_band_zero, 1)
            g.memset(neg_half[:], -0.5).then_inc(s_neg_half, 1)
            g.iota(rank_i[:], pattern=[[-1, E]], base=E, channel_multiplier=0).then_inc(s_rank_i, 1)
            pool.wait_ge(s_ones, 1)
            g.affine_select(out=ident[:], in_=ones[:], compare_op=ALU.is_equal, fill=0.0, base=0,
                            pattern=[[-1, P]], channel_multiplier=1).then_inc(s_ident, 1)
            pool.wait_ge(s_band_zero, 1)
            g.affine_select(out=band4[:], in_=band4[:], compare_op=ALU.is_ge, fill=MASKED, base=BAND,
                            pattern=[[0, J], [1, S]], channel_multiplier=-1).then_inc(s_band_half, 1)
            pool.wait_ge(s_band_half, 1)
            g.affine_select(out=band4[:], in_=band4[:], compare_op=ALU.is_ge, fill=MASKED, base=BAND,
                            pattern=[[0, J], [-1, S]], channel_multiplier=1).then_inc(s_band, 1)
            g.iota(x2_rows[:, :, TOKEN:RW].bitcast(I32), pattern=[[S, B], [0, 1]], base=0, channel_multiplier=1).then_inc(s_token, 1)
            g.memset(pad[:, 0:TOKEN], 0.0).then_inc(s_pad, 1)
            g.iota(pad[:, TOKEN:RW].bitcast(I32), pattern=[[0, 1]], base=NO_TOKEN, channel_multiplier=0).then_inc(s_pad, 1)
            g.memset(ones_bf[:], 1.0).then_inc(s_sort_half, 1)
            g.iota(sizes_i[:], pattern=[[P, B]], base=0, channel_multiplier=0).then_inc(s_sort_half, 1)
            g.iota(blocks_i[:], pattern=[[1, 16]], base=0, channel_multiplier=0).then_inc(s_sort_half, 1)
            g.memset(slots_below[:], float(P)).then_inc(s_sort_half, 1)
            pool.wait_ge(s_rank_i, 1)
            g.tensor_copy(rank[:], rank_i[:]).then_inc(s_rank, 1)
            pool.wait_ge(s_sort_half, 4)
            g.affine_select(out=before[:], in_=ones_bf[:], compare_op=ALU.is_ge, fill=0.0, base=-1,
                            pattern=[[1, P]], channel_multiplier=-1).then_inc(s_sort, 1)
            g.tensor_copy(sizes[:], sizes_i[:]).then_inc(s_sort, 1)
            g.tensor_copy(blocks[:], blocks_i[:]).then_inc(s_sort, 1)
            g.affine_select(out=slots_below[:], in_=slots_below[:], compare_op=ALU.is_ge, fill=0.0, base=-1,
                            pattern=[[1, E], [-1, E]], channel_multiplier=0).then_inc(s_sort, 1)

            def spread_keys(c, b, slot):
                for j in range(J):
                    last = g.tensor_scalar(c.kx[:, slot, :, j, :], c.ks[:, :, b, 0:c.n_keys],
                                           head_mask[:, j:j + 1], 1.0, ALU.mult, ALU.mult)
                last.then_inc(c.s_kx, 1)

            def rows(c):
                def row_values(b):
                    if b == 0:
                        pool.wait_ge(c.s_v_all, 2)
                    if b >= 2:
                        pool.wait_ge(c.s_av_ps, 2 * b - 2)
                    copy(c.v[:, b % 2, :, 0:HD], c.v_all[:, b, :].rearrange("p (h d) -> p h d", d=HD)).then_inc(c.s_v, 1)

                for b in range(B):
                    if b % ROWS == 0:
                        pool.wait_ge(c.s_rep_act, c.ready[b // ROWS] // 2)
                        pool.wait_ge(c.s_rep_dve, c.ready[b // ROWS] // 2)
                    if b >= 2:
                        pool.wait_ge(c.s_scores, 2 * b - 2)
                    spread_keys(c, b, b % 2)
                    copy(c.qs[:, b % 2], qs_all[:, :, b, :]).then_inc(c.s_qs, 1)
                    if b >= 1:
                        row_values(b - 1)
                row_values(B - 1)

            def residual(c):
                g.tensor_tensor(x_bo[:], c.x[:], bias_rows[:, c.bias_at + 1, :].unsqueeze(1).broadcast_to([S, B, D]), ALU.add).then_inc(c.s_x_bo, 1)

            def power(c):
                for half in range(2):
                    r = slice(ROWS * half, ROWS * half + ROWS)
                    pool.wait_ge(c.s_var_eps, half + 1)
                    g.tensor_tensor(rstd[:, r], var_eps[:, r], neg_half[:], ALU.pow).then_inc(c.s_rstd, 1)

            pool.wait_ge(s_head_mask, 1)
            pool.wait_ge(s_ones_col, 1)
            rows(self_)
            pool.wait_ge(s_small, 16 * 5)
            residual(self_)
            power(self_)
            pool.wait_ge(s_w_late, 16 * 7)
            rows(cross)
            residual(cross)
            power(cross)
            pool.wait_ge(s_prefilled, 16)
            pool.wait_ge(s_slot_of, 1)
            pool.wait_ge(s_gate, 1)
            pool.wait_ge(s_token, 1)
            pool.wait_ge(cross.s_normed, 2)
            for b in range(B):
                g.indirect_dma_start(slots[:, :], bass.IndirectOffsetOnAxis(ap=slot_of[:, b:b + 1], axis=0), x2_rows[:, b, :], None).then_inc(s_sorted, 16)

            out_rows = out.rearrange("b s d -> (b s) d")
            def rows_out(j):
                pool.wait_ge(s_fin, j + 1)
                g.indirect_dma_start(out_rows, bass.IndirectOffsetOnAxis(ap=xin[:, j, TOKEN:RW].bitcast(U32), axis=0), normed[:, j, :], None,
                                     bounds_check=B * S - 1, oob_is_err=False).then_inc(s_out, 16)

            for j in range(NB):
                pool.wait_ge(s_fin_var, j + 1)
                g.tensor_tensor(rstd[:, j % 2:j % 2 + 1], var_eps[:, j % 2:j % 2 + 1], neg_half[:, 0:1], ALU.pow).then_inc(s_fin_rstd, 1)
                if j >= 1:
                    rows_out(j - 1)
            rows_out(NB - 1)
            pool.wait_ge(s_out, 16 * NB)

        @block.tensor
        def _(pe):
            mm, tr = nc.tensor.matmul, nc.tensor.transpose

            def features_first(x, to_banks, s, s_ready=None):
                for b in range(B):
                    if s_ready and b % ROWS == 0:
                        pe.wait_ge(s_ready, b // ROWS + 1)
                    last = tr(bank(to_banks[b // ROWS])[:, (b % ROWS) * S:(b % ROWS + 1) * S], x[:, b, :], ident[:])
                    if b % ROWS == ROWS - 1:
                        last.then_inc(s, 1)

            def project(w, x_t, width, banks, s, s_xt=None):
                for half in range(2):
                    if s_xt:
                        pe.wait_ge(s_xt[half], 1)
                    mm(bank(banks[half])[:, 0:ROWS * width], w, x_t[:, ROWS * half:ROWS * half + ROWS, :].rearrange("p b s -> p (b s)"),
                       start=True, stop=True).then_inc(s, 1)

            def project_values(c, banks):
                for b in range(B):
                    last = mm(bank(banks[b // ROWS])[0:c.n_keys, (b % ROWS) * D:(b % ROWS + 1) * D], c.kv_t[:, b, 0:c.n_keys], c.w[2],
                              start=True, stop=True)
                    if b % ROWS == ROWS - 1:
                        last.then_inc(c.s_v_ps, 1)

            def operands(c):
                for n, of_keys, half, g, to_bank in steps(c):
                    parts, names, width = (k_parts, ("k1", "k2"), c.kp) if of_keys else (q_parts, ("q1", "q2"), S)
                    if c.masked:
                        if n == 0:
                            pe.wait_ge(c.s_q_part2, 1)
                        if n == G:
                            pe.wait_ge(c.s_q_part2, 2)
                            pe.wait_ge(c.s_k_part2, 2)
                        if n == 2 * G:
                            pe.wait_ge(c.s_rep_act, 1)
                            pe.wait_ge(c.s_rep_dve, 1)
                            project_values(c, (6, 7))
                        if n == 3 * G + 2:
                            pe.wait_ge(c.s_v_all, 2)
                    else:
                        if n == 0:
                            pe.wait_ge(c.s_k_part2, 2)
                            pe.wait_ge(c.s_v_all, 2)
                        if n == G:
                            pe.wait_ge(c.s_q_part2, 2)
                    if n >= 8:
                        step = (n - c.first_bank) % 8
                        pe.wait_ge(c.s_rep_dve if step % 2 else c.s_rep_act, step // 2 + 1)
                    for i in range(2):
                        last = mm(bank(to_bank)[:, 0:ROWS * width], sel[names[i]][:, g, :, :].rearrange("p t r -> p (t r)"),
                                  parts[i][:, ROWS * half * width:ROWS * (half + 1) * width], start=i == 0, stop=i == 1)
                    last.then_inc(c.s_rep_ps, 1)

            def scores(c, b, half, slot):
                if half == 0:
                    pe.wait_ge(c.s_qs, b + 1)
                    pe.wait_ge(c.s_kx, b + 1)
                for n in range(2):
                    g = 2 * half + n
                    o = bank(g)[:, 0:J * c.n_keys]
                    last = mm(o, c.qs[:, slot, g, :], c.kx[:, slot, g, :, :].rearrange("p j k -> p (j k)"), start=True, stop=not c.masked)
                    if c.masked:
                        last = mm(o, ident_bf[:], band4[:].rearrange("p j k -> p (j k)"), start=False, stop=True)
                last.then_inc(c.s_scores, 1)

            def transposed(c, b, half, n):
                g = 2 * half + n
                for j in range(J):
                    last = tr(bank(PT + n)[0:c.n_keys, j * S:(j + 1) * S], c.prob[:, g * J + j, :], ident[:])
                last.then_inc(c.s_prob_t_ps, 1)

            def values(c, b, half, slot, n):
                g = 2 * half + n
                pe.wait_ge(c.s_prob_t, 4 * b + g + 1)
                for j in range(J):
                    last = mm(bank(AV + slot)[32 * j:32 * j + 32, g * S:(g + 1) * S], c.v[:, slot, g * J + j, :], c.prob_t[:, g, j, :],
                              start=True, stop=True, tile_position=(0, 32 * j))
                if n == 1:
                    last.then_inc(c.s_av_ps, 1)

            def back(c, k):
                for b in range(CH * k, CH * k + CH):
                    pe.wait_ge(c.s_av, b + 1)
                    if k >= 2 and b % CH == 0:
                        pe.wait_ge(c.s_att, k - 1)
                    for g in range(G):
                        last = tr(bank(b % 4)[:, g * S:(g + 1) * S], av_all[:, b, g * S:(g + 1) * S], ident[:])
                last.then_inc(c.s_back, 1)

            def residual(c, half):
                pe.wait_ge(c.s_x_bo, 1)
                pe.wait_ge(c.s_av, B - 1 + half)
                mm(bank(6 + half), ident[:], x_bo[:, ROWS * half:ROWS * half + ROWS, :].rearrange("p b d -> p (b d)"), start=True, stop=False)

            def rows(c):
                def row(b, slot, first=False, following=True):
                    for half in range(2):
                        if following:
                            pe.wait_ge(c.s_shifted, 2 * b + half + 1)
                            scores(c, b + 1, half, 1 - slot)
                        elif half == 1:
                            back(c, 0)
                        pe.wait_ge(c.s_prob, 2 * b + half + 1)
                        if half == 1:
                            pe.wait_ge(c.s_v, b + 1)
                        for n in range(2):
                            if half == 1 or not first:
                                pe.wait_ge(c.s_prob_t, 4 * b + 2 * half + n - 1)
                            transposed(c, b, half, n)
                            if half == 1:
                                values(c, b, 0, slot, n)
                            elif not first:
                                values(c, b - 1, 1, 1 - slot, n)

                row(0, 0, first=True)
                with pe.Fori(0, B // 2 - 1) as p:
                    row(2 * p + 1, 1)
                    row(2 * p + 2, 0)
                row(B - 1, 1, following=False)
                residual(c, 0)
                for n in range(2):
                    values(c, B - 1, 1, 1, n)

            def first_scores(c):
                if c.masked:
                    pe.wait_ge(s_band, 1)
                scores(c, 0, 0, 0)
                scores(c, 0, 1, 0)

            def output(c):
                def features(k):
                    pe.wait_ge(c.s_att, k + 1)
                    if k == 0:
                        pe.wait_ge(c.s_prob_t, 4 * B)
                    if k == 1 and c.masked:
                        pe.wait_ge(s_wt_sb, 1)
                    if k >= 2:
                        pe.wait_ge(c.s_att_t, k - 1)
                    for b in range(CH * k, CH * k + CH):
                        last = tr(bank(4 + k % 2)[:, (b % CH) * S:(b % CH + 1) * S], att[:, b, :], ident[:])
                    last.then_inc(c.s_att_t_ps, 1)

                def project_out(k):
                    pe.wait_ge(c.s_att_t, k + 1)
                    for b in range(CH * k, CH * k + CH):
                        last = mm(bank(6 + b // ROWS)[:, (b % ROWS) * D:(b % ROWS + 1) * D], att_t[:, b, :], c.w[3],
                                  start=False, stop=b % ROWS == ROWS - 1)
                    if k % 2:
                        last.then_inc(c.s_out_ps, 1)

                back(c, 1)
                if c.masked:
                    pe.wait_ge(s_w_cross, 64)
                    pe.wait_ge(c.s_prob_t, 4 * B)
                    for i in range(4):
                        last = tr(bank(5)[:, i * D:(i + 1) * D], w_cross[:, i, :], ident[:])
                    last.then_inc(s_wt_ps, 1)
                for k in range(CH):
                    features(k)
                    back(c, k + 2)
                project_out(0)
                project_out(1)
                residual(c, 1)
                features(2)
                features(3)
                project_out(2)
                project_out(3)

            def keep_clock(b, n):
                for _ in range(n):
                    mm(bank(b)[:, 0:P], ones[:], ones[:], start=True, stop=True)

            pe.wait_ge(s_ones, 1)
            keep_clock(7, 9)
            pe.wait_ge(s_ident, 1)
            pe.wait_ge(s_x, 32)
            features_first(x0, (0, 1), self_.s_xt_ps)
            keep_clock(7, 4)
            for half in range(2):
                pe.wait_ge(self_.s_xt[half], 1)
            pe.wait_ge(s_w_qkv, 16)
            project(self_.w[0], xt, S, (2, 3), self_.s_q_ps)
            project(self_.w[1], xt, S, (4, 5), self_.s_k_ps)
            pe.wait_ge(s_sel, 4)
            operands(self_)
            pe.wait_ge(self_.s_rep_act, 8)
            pe.wait_ge(self_.s_rep_dve, 8)
            first_scores(self_)
            pe.wait_ge(s_context, 16)
            pe.wait_ge(s_w_late, 16 * 7)
            for b in range(B):
                last = tr(bank(4 + b // ROWS)[:, (b % ROWS) * SKP:(b % ROWS) * SKP + SK], context[:, b, :], ident[0:SK, 0:SK])
            tr(bank(5)[:, ROWS * SKP:ROWS * SKP + E * FC], b1_rows[:], ident[0:E * FC, 0:E * FC]).then_inc(s_context_t_ps, 1)
            pe.wait_ge(s_context_t, 1)
            pe.wait_ge(s_b1_sb, 1)
            rows(self_)
            output(self_)
            pe.wait_ge(s_wt_sb, 1)
            project(cross.w[1], context_t, SKP, (0, 1), cross.s_k_ps)
            project_values(cross, (2, 3))
            keep_clock(4, 5)
            features_first(x1, (4, 5), cross.s_xt_ps, self_.s_normed)
            project(cross.w[0], xt, S, (6, 7), cross.s_q_ps, cross.s_xt)
            operands(cross)
            pe.wait_ge(cross.s_rep_act, 8)
            pe.wait_ge(cross.s_rep_dve, 8)
            first_scores(cross)
            rows(cross)
            output(cross)
            keep_clock(4, 8)
            features_first(x2, (0, 1), s_x2_t_ps, cross.s_normed)

            for b in range(B):
                if b % ROWS == 0:
                    pe.wait_ge(s_x2_t[b // ROWS], 1)
                last = mm(bank(2)[:, b * E:(b + 1) * E], x2_t[:, b, :], gate_w[:], start=True, stop=True)
            last.then_inc(s_logits_ps, 1)
            flat = lambda first, end: chosen[:, first:end, :].rearrange("p b e -> p (b e)")
            pe.wait_ge(s_chosen, 2)
            pe.wait_ge(s_sort, 4)
            for back in range(1, B + 1):
                last = mm(bank(3)[:, 0:(B + 1) * E], ones_bf[:], flat(B - back, 2 * B + 1 - back), start=back == 1, stop=back == B)
                if back == 1:
                    mm(bank(3)[:, 0:B * E], before[:], flat(B, 2 * B), start=False, stop=False)
            last.then_inc(s_place_ps, 1)
            def features_of_blocks(q):
                for s_load, (first, end) in zip(s_xin, LOADS):
                    if first in QUADS[q]:
                        pe.wait_ge(s_load, 16)
                for i, j in enumerate(QUADS[q]):
                    last = tr(bank(quad_banks[q])[:, i * P:(i + 1) * P], xin[:, j, 0:D], ident[:])
                last.then_inc(s_xin_t_ps, 1)

            def up(j, slot):
                pe.wait_ge(s_cur, j + 1)
                for c in range(FC):
                    last = mm(bank(2 * slot + c // 2)[:, c % 2 * P:(c % 2 + 1) * P], w1_cur[:, slot, c * P:(c + 1) * P],
                              xin_t[:, j, :], start=True, stop=True)
                    if c % 2:
                        last.then_inc(s_up_ps, 1)

            def down(j, slot, first=False):
                e = experts[j]
                if not first:
                    pe.wait_ge(s_gated, j - 1)
                for c in range(FC):
                    if c % 2 == 0:
                        pe.wait_ge(s_hid, 2 * j + c // 2 + 1)
                    last = mm(bank(4 + slot)[:, 0:D], hid[:, slot, c, :], w2_all[:, bass.ds(e, 1), c, :].rearrange("p a n -> p (a n)"),
                              start=c == 0, stop=c == FC - 1)
                last.then_inc(s_down_ps, 1)

            pe.wait_ge(s_w2_all, 16)
            pe.wait_ge(s_expert_of, 1)
            experts = [pe.value_load(expert_of[0:1, j:j + 1], min_val=0, max_val=E - 1) for j in range(NB)]
            keep_clock(2, 8)
            features_of_blocks(0)
            pe.wait_ge(s_xin_t[0], 1)
            up(0, 0)
            for q in range(1, len(QUADS)):
                features_of_blocks(q)
            for j in range(1, NB):
                up(j, j % 2)
                if j == 1:
                    for q in range(1, len(QUADS)):
                        pe.wait_ge(s_xin_t[q], 1)
                down(j - 1, (j - 1) % 2, first=j <= 2)
            down(NB - 1, 0)

        @block.scalar
        def _(act):
            copy = lambda o, i: nc.scalar.activation(o, i, ACT.Copy)
            act.dma_start(w_qkv[:], t["L0_attn_w_qkv"]).then_inc(s_w_qkv, 16)
            act.dma_start(context[:], t["ctx_1024"].rearrange("b s d -> s b d")).then_inc(s_context, 16)

            def first_parts(s_ps, banks, parts, width, bias, s):
                for half in range(2):
                    act.wait_ge(s_ps, half + 1)
                    nc.scalar.activation(parts[0][:, ROWS * width * half:ROWS * width * (half + 1)], bank(banks[half])[:, 0:ROWS * width],
                                         ACT.Identity, bias=bias_cols[:, bias:bias + 1]).then_inc(s, 1)

            def rows(c):
                def exps(b, half):
                    act.wait_ge(c.s_shifted, 2 * b + half + 1)
                    o = c.prob[:, 8 * half:8 * half + 8, :].rearrange("p h k -> p (h k)")
                    nc.scalar.activation(o, o, ACT.Exp, scale=c.scale).then_inc(c.s_prob, 1)

                def evacuate(b, half):
                    for n in range(2):
                        g = 2 * half + n
                        act.wait_ge(c.s_prob_t_ps, 4 * b + g + 1)
                        copy(c.prob_t[:, g, :, :].rearrange("p j s -> p (j s)"), bank(PT + n)[0:c.n_keys, :]).then_inc(c.s_prob_t, 1)

                def read_values(b, slot):
                    if not c.masked:
                        return
                    act.wait_ge(c.s_av_ps, 2 * b + 2)
                    copy(av_all[:, bass.ds(b, 1), :], bank(AV + slot).rearrange("p (a n) -> p a n", a=1)).then_inc(c.s_av, 1)

                def row(b, slot):
                    exps(b, 0)
                    evacuate(b - 1, 1)
                    exps(b, 1)
                    evacuate(b, 0)
                    read_values(b - 1, 1 - slot)

                exps(0, 0)
                exps(0, 1)
                evacuate(0, 0)
                with act.Fori(0, B // 2 - 1) as p:
                    row(2 * p + 1, 1)
                    row(2 * p + 2, 0)
                row(B - 1, 1)
                evacuate(B - 1, 1)
                read_values(B - 1, 1)

            def output(c):
                if c.masked:
                    act.wait_ge(s_wt_ps, 1)
                    copy(w_cross_t[:].rearrange("p a d -> p (a d)"), bank(5)).then_inc(s_wt_sb, 1)
                for k in range(NCH):
                    act.wait_ge(c.s_att_t_ps, k + 1)
                    copy(att_t[:, CH * k:CH * k + CH, :].rearrange("p b s -> p (b s)"), bank(4 + k % 2)[:, 0:CH * S]).then_inc(c.s_att_t, 1)

            def features_first(to, b, s_ps, s):
                act.wait_ge(s_ps, 1)
                copy(to[:, 0:ROWS, :].rearrange("p b s -> p (b s)"), bank(b)).then_inc(s[0], 1)

            act.wait_ge(s_ident, 1)
            copy(ident_bf[:], ident[:]).then_inc(s_ident_bf, 1)
            features_first(xt, 0, self_.s_xt_ps, self_.s_xt)
            act.wait_ge(s_small, 16 * 5)
            first_parts(self_.s_q_ps, (2, 3), q_parts, S, 0, self_.s_q_part1)
            first_parts(self_.s_k_ps, (4, 5), k_parts, S, 1, self_.s_k_part1)
            operands_to_sb(self_, act, copy, 0, self_.s_rep_act)
            act.wait_ge(s_context_t_ps, 1)
            for half in range(2):
                last = copy(context_t[:, ROWS * half:ROWS * half + ROWS, 0:SK],
                            bank(4 + half)[:, 0:ROWS * SKP].rearrange("p (b s) -> p b s", s=SKP)[:, :, 0:SK])
            last.then_inc(s_context_t, 1)
            copy(b1_t[:], bank(5)[:, ROWS * SKP:ROWS * SKP + E * FC]).then_inc(s_b1_sb, 1)
            rows(self_)
            output(self_)
            first_parts(cross.s_k_ps, (0, 1), k_parts, SKP, 3, cross.s_k_part1)
            for half in range(2):
                act.wait_ge(cross.s_xt_ps, half + 1)
                copy(xt[:, ROWS * half:ROWS * half + ROWS, :].rearrange("p b s -> p (b s)"), bank(4 + half)).then_inc(cross.s_xt[half], 1)
            first_parts(cross.s_q_ps, (6, 7), q_parts, S, 2, cross.s_q_part1)
            operands_to_sb(cross, act, copy, 0, cross.s_rep_act)
            rows(cross)
            output(cross)
            features_first(x2_t, 0, s_x2_t_ps, s_x2_t)

            act.wait_ge(s_route, 2)
            nc.scalar.activation(exps[:], shifted[:], ACT.Exp).then_inc(s_exps, 1)
            nc.scalar.preload_act_table(ACT.Gelu)
            act.wait_ge(s_xin_t_ps, 1)
            quad_to_sb(copy, 0)

            def hidden(j, slot):
                for c in range(FC):
                    if c % 2 == 0:
                        act.wait_ge(s_up_ps, 2 * j + 1 + c // 2)
                    last = nc.scalar.activation(hid[:, slot, c, :], bank(2 * slot + c // 2)[:, c % 2 * P:(c % 2 + 1) * P], ACT.Gelu, bias=b1_cur[:, slot, c:c + 1])
                    if c % 2:
                        last.then_inc(s_hid, 1)

            hidden(0, 0)
            act.wait_ge(s_xin_t_ps, 3)
            quad_to_sb(copy, 2)
            for j in (1, 2):
                hidden(j, j % 2)
            with act.Fori(1, NB // 2) as p:
                hidden(2 * p + 1, 1)
                hidden(2 * p + 2, 0)

        @block.vector
        def _(dve):
            v = nc.vector

            def second_parts(s_part1, banks, parts, width, bias, s):
                for half in range(2):
                    o = slice(ROWS * width * half, ROWS * width * (half + 1))
                    dve.wait_ge(s_part1, half + 1)
                    v.scalar_tensor_tensor(parts[1][:, o], bank(banks[half])[:, 0:ROWS * width], bias_cols[:, bias:bias + 1],
                                           parts[0][:, o].bitcast(F32), ALU.add, ALU.subtract).then_inc(s, 1)

            def values(c, banks):
                n = c.n_keys
                for half in range(2):
                    dve.wait_ge(c.s_v_ps, half + 1)
                    v.tensor_tensor(c.v_all[:, ROWS * half:ROWS * half + ROWS, :], bank(banks[half])[0:n, :].rearrange("p (b d) -> p b d", b=ROWS),
                                    bias_rows[0:n, c.bias_at, :].unsqueeze(1).broadcast_to([n, ROWS, D]), ALU.add).then_inc(c.s_v_all, 1)

            def normalise(c, k):
                dve.wait_ge(c.s_back, k + 1)
                r = slice(CH * k, CH * k + CH)
                first = CH * k % 4
                back = ps[:, first:first + CH, :].rearrange("p b (h w) -> p b h w", w=32)
                v.reciprocal(rden[:, r, :].unsqueeze(3), back[:, :, :, HD:HD + 1]).then_inc(c.s_rden, 1)
                dve.wait_ge(c.s_rden, k + 1)
                v.tensor_tensor(att[:, r, :].rearrange("p b (h d) -> p b h d", d=HD), back[:, :, :, 0:HD],
                                rden[:, r, :].unsqueeze(3).broadcast_to([S, CH, H, HD]), ALU.mult).then_inc(c.s_att, 1)

            def rows(c):
                def half_row(b, half, first=False):
                    dve.wait_ge(c.s_scores, 2 * b + half + 1)
                    sc = ps[:, 2 * half:2 * half + 2, 0:J * c.n_keys].rearrange("p g (j k) -> p g j k", j=J)
                    m = mx[:, 8 * half:8 * half + 8].rearrange("p (g j) -> p g j", j=J)
                    v.tensor_reduce(m, sc, AX.X, ALU.max).then_inc(c.s_mx, 1)
                    dve.wait_ge(c.s_mx, 2 * b + half + 1)
                    if not first:
                        dve.wait_ge(c.s_prob_t_ps, 4 * b + 2 * half - 2)
                    o = c.prob[:, 8 * half:8 * half + 8, :].rearrange("p (g j) k -> p g j k", j=J)
                    v.tensor_tensor(o, sc, m.unsqueeze(3).broadcast_to([S, 2, J, c.n_keys]), ALU.subtract).then_inc(c.s_shifted, 1)

                def read_values(b, slot):
                    dve.wait_ge(c.s_av_ps, 2 * b + 2)
                    v.tensor_copy(av_all[:, bass.ds(b, 1), :], bank(AV + slot).rearrange("p (a n) -> p a n", a=1)).then_inc(c.s_av, 1)

                def row(b, slot, first=False):
                    half_row(b, 0)
                    if not c.masked and not first:
                        read_values(b - 2, slot)
                    half_row(b, 1)

                for half in range(2):
                    half_row(0, half, first=True)
                row(1, 1, first=True)
                with dve.Fori(1, B // 2) as p:
                    row(2 * p, 0)
                    row(2 * p + 1, 1)
                if not c.masked:
                    read_values(B - 2, 0)
                normalise(c, 0)
                if not c.masked:
                    read_values(B - 1, 1)

            def output(c):
                for k in range(1, NCH):
                    normalise(c, k)
                summed = ps[:, 6:8, :].rearrange("p h (b d) -> p (h b) d", d=D)
                for half in range(2):
                    dve.wait_ge(c.s_out_ps, half + 1)
                    layer_stats(summed, half, c.s_stats, c.s_mv, c.s_var_eps)
                for half in range(2):
                    dve.wait_ge(c.s_rstd, half + 1)
                    layer_norm(c.to, summed, half, c.s_normed)

            def layer_stats(a, half, s_stats, s_mv, s_var_eps):
                rs_ = range(ROWS * half, ROWS * half + ROWS)
                for b in rs_:
                    last = v.bn_stats(stats[:, b, :], a[:, b, :])
                last.then_inc(s_stats, 1)
                dve.wait_ge(s_stats, half + 1)
                for b in rs_:
                    last = v.bn_aggr(mv[:, b, :], stats[:, b, :])
                last.then_inc(s_mv, 1)
                dve.wait_ge(s_mv, half + 1)
                r = slice(ROWS * half, ROWS * half + ROWS)
                v.tensor_scalar(var_eps[:, r].unsqueeze(2), mv[:, r, 1:2], EPS, None, ALU.add).then_inc(s_var_eps, 1)

            def layer_norm(to, a, half, s):
                for b in range(ROWS * half, ROWS * half + ROWS):
                    last = v.tensor_scalar(to[:, b, :], a[:, b, :], mv[:, b, 0:1], rstd[:, b:b + 1], ALU.subtract, ALU.mult)
                last.then_inc(s, 1)

            def features_first(to, b, s_ps, s):
                dve.wait_ge(s_ps, 2)
                v.tensor_copy(to[:, ROWS:B, :].rearrange("p b s -> p (b s)"), bank(b)).then_inc(s[1], 1)

            v.memset(v_row[:], 0.0).then_inc(s_zeroed, 1)
            v.memset(chosen[:, 0:B, :], 0.0).then_inc(s_chosen, 1)
            v.memset(context_t[:, :, SK:], 0.0).then_inc(s_zeroed, 1)
            for n in sel_names:
                v.memset(sel[n][:].bitcast(F32), 0.0).then_inc(s_zeroed, 1)
            dve.wait_ge(s_zeroed, 6)
            v.memset(v_row[:, :, :, HD:HD + 1], 1.0).then_inc(s_ones_col, 1)
            dve.wait_ge(s_ident, 1)
            by_group = ident[:].rearrange("p (g r) -> p g r", r=R)
            for n, quadrants in zip(sel_names, ((0, 1), (2, 3), (0, 2), (1, 3))):
                for q in quadrants:
                    last = v.tensor_copy(sel[n][:, :, q, :], by_group)
                last.then_inc(s_sel, 1)
            v.tensor_reduce(head_mask[:], ident[:].rearrange("p (q j d) -> p j q d", q=4, d=HD), AX.XY, ALU.add).then_inc(s_head_mask, 1)

            features_first(xt, 1, self_.s_xt_ps, self_.s_xt)
            dve.wait_ge(s_small, 16 * 5)
            second_parts(self_.s_q_part1, (2, 3), q_parts, S, 0, self_.s_q_part2)
            second_parts(self_.s_k_part1, (4, 5), k_parts, S, 1, self_.s_k_part2)
            operands_to_sb(self_, dve, v.tensor_copy, 1, self_.s_rep_dve, values=lambda: values(self_, (6, 7)))
            rows(self_)
            output(self_)
            dve.wait_ge(s_w_late, 16 * 7)
            second_parts(cross.s_k_part1, (0, 1), k_parts, SKP, 3, cross.s_k_part2)
            values(cross, (2, 3))
            second_parts(cross.s_q_part1, (6, 7), q_parts, S, 2, cross.s_q_part2)
            operands_to_sb(cross, dve, v.tensor_copy, 1, cross.s_rep_dve)
            rows(cross)
            output(cross)
            features_first(x2_t, 1, s_x2_t_ps, s_x2_t)

            per_token = lambda a: a[:].unsqueeze(2).broadcast_to([P, B, E])
            per_expert = lambda a: a.unsqueeze(1).broadcast_to([P, B, E])
            dve.wait_ge(s_logits_ps, 1)
            logits = bank(2)[:, 0:B * E].rearrange("p (b e) -> p b e", e=E)
            v.tensor_reduce(top[:], logits, AX.X, ALU.max).then_inc(s_route, 1)
            dve.wait_ge(s_route, 1)
            v.tensor_tensor(shifted[:], logits, per_token(top), ALU.subtract).then_inc(s_route, 1)
            dve.wait_ge(s_rank, 1)
            dve.wait_ge(s_route, 2)
            v.scalar_tensor_tensor(ranked[:], shifted[:], 0.0, per_expert(rank[:]), ALU.is_equal, ALU.mult).then_inc(s_route, 1)
            dve.wait_ge(s_route, 3)
            v.tensor_reduce(top_rank[:], ranked[:], AX.X, ALU.max).then_inc(s_route, 1)
            dve.wait_ge(s_route, 4)
            v.tensor_tensor(chosen[:, B:, :], ranked[:], per_token(top_rank), ALU.is_equal).then_inc(s_chosen, 1)
            dve.wait_ge(s_exps, 1)
            v.tensor_reduce(sum_exps[:], exps[:], AX.X, ALU.add).then_inc(s_route, 1)
            dve.wait_ge(s_route, 5)
            v.reciprocal(x2_rows[:, :, GATE:TOKEN], sum_exps[:].unsqueeze(2)).then_inc(s_gate, 1)
            dve.wait_ge(s_place_ps, 1)
            v.tensor_tensor(reaches[:], bank(3)[:, B * E:(B + 1) * E].unsqueeze(2).broadcast_to([P, E, B]),
                            sizes[:].unsqueeze(1).broadcast_to([P, E, B]), ALU.is_gt).then_inc(s_route, 1)
            dve.wait_ge(s_route, 6)
            v.tensor_reduce(n_blocks[:], reaches[:], AX.X, ALU.add).then_inc(s_route, 1)
            dve.wait_ge(s_route, 7)
            v.tensor_tensor(below[:], slots_below[:], per_expert(n_blocks[:]), ALU.mult).then_inc(s_route, 1)
            dve.wait_ge(s_route, 8)
            v.tensor_reduce(first_slot[:], below[:], AX.X, ALU.add).then_inc(s_route, 1)
            dve.wait_ge(s_route, 9)
            v.tensor_tensor(place[:], bank(3)[:, 0:B * E].rearrange("p (b e) -> p b e", e=E), per_expert(first_slot[:]), ALU.add).then_inc(s_route, 1)
            v.scalar_tensor_tensor(end_block[:], first_slot[:], 1.0 / P, n_blocks[:], ALU.mult, ALU.add).then_inc(s_route, 1)
            dve.wait_ge(s_route, 10)
            v.tensor_tensor(ranked[:], place[:], chosen[:, B:, :], ALU.mult).then_inc(s_route, 1)
            dve.wait_ge(s_route, 11)
            v.tensor_tensor(ended[:], blocks[0:1, :].unsqueeze(2).broadcast_to([1, 16, E]),
                            end_block[0:1, :].unsqueeze(1).broadcast_to([1, 16, E]), ALU.is_ge).then_inc(s_route, 1)
            dve.wait_ge(s_route, 12)
            v.tensor_reduce(top[:], ranked[:], AX.X, ALU.add).then_inc(s_route, 1)
            dve.wait_ge(s_route, 14)
            v.tensor_copy(slot_of[:], top[:]).then_inc(s_slot_of, 1)
            dve.wait_ge(s_route, 13)
            v.tensor_reduce(n_ended[:], ended[:], AX.X, ALU.add).then_inc(s_route, 1)
            dve.wait_ge(s_route, 15)
            v.tensor_scalar(expert_of[:], n_ended[:], float(E - 1), None, ALU.min).then_inc(s_expert_of, 1)

            row = lambda a: a.rearrange("p a n -> p (a n)")

            def load_w1(j, slot):
                v.tensor_copy(w1_cur[:, slot, :], row(w1_all[:, bass.ds(experts[j], 1), :]))

            def load_b1(j, slot):
                v.tensor_copy(b1_cur[:, slot, :], b1_t[:, bass.ds(experts[j] * FC, FC)]).then_inc(s_cur, 1)

            def add_b2(j):
                if j % 4 == 0:
                    dve.wait_ge(s_xin_t_ps, j // 4 + 1)
                v.scalar_tensor_tensor(xin[:, j, 0:D], row(b2_all[:, bass.ds(experts[j], 1), :]), xin[:, j, GATE:TOKEN],
                                       xin[:, j, 0:D], ALU.mult, ALU.add).then_inc(s_plus_b2, 1)

            def block_out(j, slot, loads, first=False):
                if loads:
                    dve.wait_ge(s_up_ps, 2 * j + 2)
                    load_w1(j + 2, slot)
                if not first:
                    dve.wait_ge(s_fin_stats, j)
                    v.bn_aggr(mv[:, 1 - slot, :], stats[:, 1 - slot, :]).then_inc(s_fin_mv, 1)
                if loads:
                    dve.wait_ge(s_hid, 2 * j + 2)
                    load_b1(j + 2, slot)
                if not first:
                    variance(j - 1, 1 - slot)
                if loads:
                    add_b2(j + 2)
                dve.wait_ge(s_plus_b2, j + 1)
                dve.wait_ge(s_down_ps, j + 1)
                v.scalar_tensor_tensor(gated[:, slot, :], bank(4 + slot)[:, 0:D], xin[:, j, GATE:TOKEN], xin[:, j, 0:D],
                                       ALU.mult, ALU.add).then_inc(s_gated, 1)
                if not first:
                    normalise_block(j - 1, 1 - slot)
                dve.wait_ge(s_gated, j + 1)
                v.bn_stats(stats[:, slot, :], gated[:, slot, :]).then_inc(s_fin_stats, 1)

            def variance(j, slot):
                dve.wait_ge(s_fin_mv, j + 1)
                v.tensor_scalar(var_eps[:, slot:slot + 1], mv[:, slot, 1:2], EPS, None, ALU.add).then_inc(s_fin_var, 1)

            def normalise_block(j, slot):
                dve.wait_ge(s_fin_rstd, j + 1)
                v.tensor_scalar(normed[:, j, :], gated[:, slot, :], mv[:, slot, 0:1],
                                rstd[:, slot:slot + 1], ALU.subtract, ALU.mult).then_inc(s_fin, 1)

            dve.wait_ge(s_expert_of, 1)
            dve.wait_ge(s_w1_all, 16)
            experts = [dve.value_load(expert_of[0:1, j:j + 1], min_val=0, max_val=E - 1) for j in range(NB)]
            for j in range(2):
                load_w1(j, j)
                load_b1(j, j)
            for q in range(1, len(QUADS), 2):
                dve.wait_ge(s_xin_t_ps, q + 1)
                quad_to_sb(v.tensor_copy, q)
            for j in range(2):
                add_b2(j)
            block_out(0, 0, loads=True, first=True)
            for j in range(1, NB):
                block_out(j, j % 2, loads=j + 2 < NB)
            dve.wait_ge(s_fin_stats, NB)
            v.bn_aggr(mv[:, 0, :], stats[:, 0, :]).then_inc(s_fin_mv, 1)
            variance(NB - 1, 0)
            normalise_block(NB - 1, 0)


_INS = ['x', 'ctx_1024', 'L0_attn_w_qkv', 'L0_attn_b_qkv', 'L0_attn_w_out', 'L0_attn_b_out', 'L0_xattn_Wq', 'L0_xattn_bq',
        'L0_xattn_Wk', 'L0_xattn_bk', 'L0_xattn_Wv', 'L0_xattn_bv', 'L0_xattn_Wo', 'L0_xattn_bo', 'L0_ffn_gate_w',
        'L0_ffn_w1', 'L0_ffn_b1', 'L0_ffn_w2', 'L0_ffn_b2']


def kernel(**inputs):
    import numpy as _np
    import concourse.bacc as _bacc
    from concourse import mybir as _mybir
    from concourse.bass_utils import run_bass_kernel_spmd as _run

    nc = _bacc.Bacc("TRN2", target_bir_lowering=False, num_devices=1)
    arrays, aps = {}, {}
    for name in _INS:
        a = _np.ascontiguousarray(inputs[name])
        arrays[f"in_{name}"] = a
        aps[name] = nc.dram_tensor(f"in_{name}", a.shape, _mybir.dt.from_np(a.dtype), kind="ExternalInput").ap()
    out = nc.dram_tensor("out_0", (B, S, D), F32, kind="ExternalOutput").ap()
    slots = nc.dram_tensor("slots", (NB * P, RW), F32, kind="Internal").ap()
    build(nc, aps, out, slots)
    r = _run(nc, [arrays], core_ids=[0])
    return r.results[0]["out_0"]
```
